# Optimizing a Trainium2 kernel written in Bass

```python
import numpy as np
import jax
import jax.numpy as jnp

def _softmax(x, axis=-1):
    return jax.nn.softmax(x, axis=axis)

def _gelu(x):
    return jax.nn.gelu(x, approximate=True)

def _silu(x):
    return jax.nn.silu(x)

def _sigmoid(x):
    return jax.nn.sigmoid(x)

def _layernorm(x, axis=-1, eps=1e-05):
    m = jnp.mean(x, axis=axis, keepdims=True)
    v = jnp.var(x, axis=axis, keepdims=True)
    return (x - m) / jnp.sqrt(v + eps)

def _scatter_add(tgt, idx, src, axis=0):
    return tgt.at[idx].add(src)

def _segment_sum(src, seg, n):
    return jax.ops.segment_sum(src, seg, n)
kernel_name = 'mk_cond_seq_d4_seqx_r8_a7887d'

def setup_inputs(seed: int=0):
    np.random.seed(seed)
    _w = jnp.asarray

    def _rec_inputs():
        import jax
        import jax.numpy as jnp
        _rk = jax.random.key(seed)
        x = -7.109e-05 + 0.9999 * jax.random.normal(jax.random.fold_in(_rk, 1), (128, 32, 128), jnp.float32)
        _lenS = 32 - jax.random.randint(jax.random.fold_in(_rk, 7), (128,), 0, max(1, 32 // 4) + 1, jnp.int32)
        _lenS2 = 32 - jax.random.randint(jax.random.fold_in(_rk, 8), (128,), 0, max(1, 32 // 4) + 1, jnp.int32)
        condB_theta = jax.random.uniform(jax.random.fold_in(_rk, 11), (128,), jnp.float32, 0.0, 0.983423)
        condB_phi = jax.random.uniform(jax.random.fold_in(_rk, 12), (128,), jnp.float32, 0.0, 0.961312)
        itok_B_0_7 = jax.random.randint(jax.random.fold_in(_rk, 13), (128,), 0, 8, jnp.int32)
        itok_B_0_15 = jax.random.randint(jax.random.fold_in(_rk, 14), (128,), 0, 16, jnp.int32)
        condB_safetyscore = -0.927215 + 0.920279 * jax.random.normal(jax.random.fold_in(_rk, 15), (128,), jnp.float32)
        return (x, condB_theta, condB_phi, itok_B_0_7, itok_B_0_15, condB_safetyscore)
    x, condB_theta, condB_phi, itok_B_0_7, itok_B_0_15, condB_safetyscore = _rec_inputs()

    def _L0_cond_setup():
        import jax, jax.numpy as jnp
        import numpy as np
        key = jax.random.key(seed)
        k1, k2, k3 = jax.random.split(key, 3)
        B, N, D = (16, 512, 128)
        embeddings = jax.random.normal(k1, (B, N, D), dtype=jnp.float32)
        theta = jax.random.uniform(k2, (B,), dtype=jnp.float32)
        phi = jax.random.uniform(k3, (B,), dtype=jnp.float32)
        return {'embeddings': embeddings, 'theta': theta, 'phi': phi}
    _L0_cond_all = _L0_cond_setup()
    _L0_cond_in = {k: v for k, v in _L0_cond_all.items() if k in ()}
    del _L0_cond_all

    def _L1_cond_setup():
        import jax, jax.numpy as jnp
        import numpy as np
        E, H, I = (8, 128, 512)
        B, S = (4, 128)
        LN_EPS = 1e-12
        key = jax.random.key(seed)
        ks = jax.random.split(key, 8)
        x = jax.random.normal(ks[0], (B, S, H), dtype=jnp.float32)
        expert_idx = jax.random.randint(ks[1], (B,), 0, E, dtype=jnp.int64)
        Wi = jax.random.normal(ks[2], (E, H, I), dtype=jnp.float32) * 0.02
        bi = jnp.zeros((E, I), dtype=jnp.float32)
        Wo = jax.random.normal(ks[3], (E, I, H), dtype=jnp.float32) * 0.02
        bo = jnp.zeros((E, H), dtype=jnp.float32)
        gamma = jnp.ones((E, H), dtype=jnp.float32)
        beta = jnp.zeros((E, H), dtype=jnp.float32)
        return {'input_tensor': x, 'expert_idx': expert_idx, 'Wi': Wi, 'bi': bi, 'Wo': Wo, 'bo': bo, 'gamma': gamma, 'beta': beta}
    _L1_cond_all = _L1_cond_setup()
    _L1_cond_in = {k: v for k, v in _L1_cond_all.items() if k in ('Wi', 'bi', 'Wo', 'bo', 'gamma', 'beta')}
    del _L1_cond_all

    def _L2_cond_setup():
        import jax, jax.numpy as jnp
        import numpy as np
        B, S, D = (32, 128, 128)
        A = 32
        E = 16
        LN_EPS = 1e-05
        key = jax.random.key(seed)
        ks = jax.random.split(key, 10)
        s = lambda fan_in: 1.0 / np.sqrt(fan_in)
        return {'hidden_states': jax.random.normal(ks[0], (B, S, D), dtype=jnp.float32), 'domain_id': jax.random.randint(ks[1], (B,), 0, E, dtype=jnp.int64), 'down_W': jax.random.uniform(ks[2], (A, D), jnp.float32, -s(D), s(D)), 'down_b': jax.random.uniform(ks[3], (A,), jnp.float32, -s(D), s(D)), 'up_W': jax.random.uniform(ks[4], (D, A), jnp.float32, -s(A), s(A)), 'up_b': jax.random.uniform(ks[5], (D,), jnp.float32, -s(A), s(A)), 'expert_W': jax.random.uniform(ks[6], (E, A, A), jnp.float32, -s(A), s(A)), 'expert_b': jax.random.uniform(ks[7], (E, A), jnp.float32, -s(A), s(A)), 'domain_emb': jax.random.normal(ks[8], (E, A), dtype=jnp.float32), 'ln_gamma': jnp.ones((D,), jnp.float32), 'ln_beta': jnp.zeros((D,), jnp.float32)}
    _L2_cond_all = _L2_cond_setup()
    _L2_cond_in = {k: v for k, v in _L2_cond_all.items() if k in ('down_W', 'down_b', 'up_W', 'up_b', 'expert_W', 'expert_b', 'domain_emb', 'ln_gamma', 'ln_beta')}
    del _L2_cond_all

    def _L3_cond_setup():
        import jax, jax.numpy as jnp
        import numpy as np
        TEMPERATURE = 1.0
        ACT_THRESHOLD = 0.1
        MAX_ACT = 1.0
        SAFETY_KNOB = 1.0
        EPS = 1e-08

        def gram_schmidt(X):
            r = X.shape[1]
            Q = X
            for i in range(r):
                q = Q[:, i]
                q = q / (jnp.linalg.norm(q) + EPS)
                Q = Q.at[:, i].set(q)
                coeffs = q @ Q[:, i + 1:]
                Q = Q.at[:, i + 1:].add(-jnp.outer(q, coeffs))
            return Q
        key = jax.random.key(seed)
        ks = jax.random.split(key, 8)
        B, S, D, R = (8, 512, 128, 32)
        init_std = 0.02
        return {'hidden_states': jax.random.normal(ks[0], (B, S, D), jnp.float32), 'safety_score': jax.random.normal(ks[1], (B,), jnp.float32), 'U': jax.random.normal(ks[2], (D, R), jnp.float32) * init_std, 'V': jax.random.normal(ks[3], (D, R), jnp.float32) * init_std, 'safety_bias': jnp.zeros((D,), jnp.float32), 'gate_w1': jax.random.normal(ks[4], (D // 4, D), jnp.float32) * (1.0 / np.sqrt(D)), 'gate_b1': jnp.zeros((D // 4,), jnp.float32), 'gate_w2': jax.random.normal(ks[5], (1, D // 4), jnp.float32) * (1.0 / np.sqrt(D // 4)), 'gate_b2': jnp.zeros((1,), jnp.float32), 'resp_w': jax.random.normal(ks[6], (D, R), jnp.float32) * (1.0 / np.sqrt(R)), 'resp_b': jnp.zeros((D,), jnp.float32)}
    _L3_cond_all = _L3_cond_setup()
    _L3_cond_in = {k: v for k, v in _L3_cond_all.items() if k in ('U', 'V', 'safety_bias', 'gate_w1', 'gate_b1', 'gate_w2', 'gate_b2', 'resp_w', 'resp_b')}
    del _L3_cond_all
    return {'x': x, 'condB_theta': condB_theta, 'condB_phi': condB_phi, 'itok_B_0_7': itok_B_0_7, 'itok_B_0_15': itok_B_0_15, 'condB_safetyscore': condB_safetyscore, 'L1_cond_Wi': _L1_cond_in['Wi'], 'L1_cond_bi': _L1_cond_in['bi'], 'L1_cond_Wo': _L1_cond_in['Wo'], 'L1_cond_bo': _L1_cond_in['bo'], 'L1_cond_gamma': _L1_cond_in['gamma'], 'L1_cond_beta': _L1_cond_in['beta'], 'L2_cond_down_W': _L2_cond_in['down_W'], 'L2_cond_down_b': _L2_cond_in['down_b'], 'L2_cond_up_W': _L2_cond_in['up_W'], 'L2_cond_up_b': _L2_cond_in['up_b'], 'L2_cond_expert_W': _L2_cond_in['expert_W'], 'L2_cond_expert_b': _L2_cond_in['expert_b'], 'L2_cond_domain_emb': _L2_cond_in['domain_emb'], 'L2_cond_ln_gamma': _L2_cond_in['ln_gamma'], 'L2_cond_ln_beta': _L2_cond_in['ln_beta'], 'L3_cond_U': _L3_cond_in['U'], 'L3_cond_V': _L3_cond_in['V'], 'L3_cond_safety_bias': _L3_cond_in['safety_bias'], 'L3_cond_gate_w1': _L3_cond_in['gate_w1'], 'L3_cond_gate_b1': _L3_cond_in['gate_b1'], 'L3_cond_gate_w2': _L3_cond_in['gate_w2'], 'L3_cond_gate_b2': _L3_cond_in['gate_b2'], 'L3_cond_resp_w': _L3_cond_in['resp_w'], 'L3_cond_resp_b': _L3_cond_in['resp_b']}

def reference(x, condB_theta, condB_phi, itok_B_0_7, itok_B_0_15, condB_safetyscore, L1_cond_Wi, L1_cond_bi, L1_cond_Wo, L1_cond_bo, L1_cond_gamma, L1_cond_beta, L2_cond_down_W, L2_cond_down_b, L2_cond_up_W, L2_cond_up_b, L2_cond_expert_W, L2_cond_expert_b, L2_cond_domain_emb, L2_cond_ln_gamma, L2_cond_ln_beta, L3_cond_U, L3_cond_V, L3_cond_safety_bias, L3_cond_gate_w1, L3_cond_gate_b1, L3_cond_gate_w2, L3_cond_gate_b2, L3_cond_resp_w, L3_cond_resp_b):
    import jax
    import jax.numpy as jnp

    def _L0_cond_ref(embeddings, theta, phi):
        import jax, jax.numpy as jnp
        import numpy as np
        B, N, D = embeddings.shape
        e = embeddings.reshape(B, N, D // 4, 4)
        ct = jnp.cos(theta)[:, None, None]
        st = jnp.sin(theta)[:, None, None]
        cp = jnp.cos(phi)[:, None, None]
        sp = jnp.sin(phi)[:, None, None]
        x0, x1, x2, x3 = (e[..., 0], e[..., 1], e[..., 2], e[..., 3])
        out = jnp.stack([x0 * ct + x1 * st, -x0 * st + x1 * ct, x2 * cp + x3 * sp, -x2 * sp + x3 * cp], axis=-1)
        return out.reshape(B, N, D)

    def _L1_cond_ref(input_tensor, expert_idx, Wi, bi, Wo, bo, gamma, beta):
        import jax, jax.numpy as jnp
        import numpy as np
        E, H, I = (8, 128, 512)
        B, S = (4, 128)
        LN_EPS = 1e-12
        Wi_b = Wi[expert_idx]
        bi_b = bi[expert_idx]
        Wo_b = Wo[expert_idx]
        bo_b = bo[expert_idx]
        g_b = gamma[expert_idx]
        be_b = beta[expert_idx]
        h = jax.nn.gelu(jnp.einsum('bsh,bhi->bsi', input_tensor, Wi_b) + bi_b[:, None, :], approximate=False)
        o = jnp.einsum('bsi,bih->bsh', h, Wo_b) + bo_b[:, None, :]
        r = o + input_tensor
        mu = jnp.mean(r, axis=-1, keepdims=True)
        var = jnp.mean(jnp.square(r - mu), axis=-1, keepdims=True)
        y = (r - mu) * jax.lax.rsqrt(var + LN_EPS)
        return y * g_b[:, None, :] + be_b[:, None, :]

    def _L2_cond_ref(hidden_states, domain_id, down_W, down_b, up_W, up_b, expert_W, expert_b, domain_emb, ln_gamma, ln_beta):
        import jax, jax.numpy as jnp
        import numpy as np
        B, S, D = (32, 128, 128)
        A = 32
        E = 16
        LN_EPS = 1e-05
        residual = hidden_states
        hidden = jnp.einsum('bsd,ad->bsa', hidden_states, down_W) + down_b
        hidden = jax.nn.gelu(hidden, approximate=False)
        valid = (domain_id >= 0) & (domain_id < E)
        idx = jnp.clip(domain_id, 0, E - 1)
        Wsel = expert_W[idx]
        bsel = expert_b[idx]
        expert_out = jnp.einsum('bsa,boa->bso', hidden, Wsel) + bsel[:, None, :]
        domain_output = jnp.where(valid[:, None, None], expert_out, hidden)
        hidden = domain_output + domain_emb[idx][:, None, :]
        hidden = jnp.einsum('bsa,da->bsd', hidden, up_W) + up_b
        x = hidden + residual
        mu = jnp.mean(x, axis=-1, keepdims=True)
        var = jnp.mean(jnp.square(x - mu), axis=-1, keepdims=True)
        return (x - mu) * jax.lax.rsqrt(var + LN_EPS) * ln_gamma + ln_beta

    def _L3_cond_ref(hidden_states, safety_score, U, V, safety_bias, gate_w1, gate_b1, gate_w2, gate_b2, resp_w, resp_b):
        import jax, jax.numpy as jnp
        import numpy as np
        TEMPERATURE = 1.0
        ACT_THRESHOLD = 0.1
        MAX_ACT = 1.0
        SAFETY_KNOB = 1.0
        EPS = 1e-08

        def gram_schmidt(X):
            r = X.shape[1]
            Q = X
            for i in range(r):
                q = Q[:, i]
                q = q / (jnp.linalg.norm(q) + EPS)
                Q = Q.at[:, i].set(q)
                coeffs = q @ Q[:, i + 1:]
                Q = Q.at[:, i + 1:].add(-jnp.outer(q, coeffs))
            return Q
        R = resp_w.shape[1]
        U_o = gram_schmidt(U)
        V_o = gram_schmidt(V)
        basis = U_o @ V_o.T
        pooled = hidden_states.mean(axis=1)
        h1 = jax.nn.relu(pooled @ gate_w1.T + gate_b1)
        base_act = jax.nn.sigmoid(h1 @ gate_w2.T + gate_b2)
        mod = jax.nn.sigmoid(safety_score[:, None] / TEMPERATURE)
        knob = jnp.clip(jnp.asarray(SAFETY_KNOB, hidden_states.dtype), ACT_THRESHOLD, MAX_ACT)
        strength = (base_act * mod * knob)[:, None, :]
        proj = hidden_states @ basis
        feats = proj @ basis.T[:, :R]
        response = feats @ resp_w.T + resp_b + safety_bias
        return hidden_states + strength * response
    x = _L0_cond_ref(x, condB_theta, condB_phi)
    x = _L1_cond_ref(x, itok_B_0_7, L1_cond_Wi, L1_cond_bi, L1_cond_Wo, L1_cond_bo, L1_cond_gamma, L1_cond_beta)
    x = _L2_cond_ref(x, itok_B_0_15, L2_cond_down_W, L2_cond_down_b, L2_cond_up_W, L2_cond_up_b, L2_cond_expert_W, L2_cond_expert_b, L2_cond_domain_emb, L2_cond_ln_gamma, L2_cond_ln_beta)
    x = _L3_cond_ref(x, condB_safetyscore, L3_cond_U, L3_cond_V, L3_cond_safety_bias, L3_cond_gate_w1, L3_cond_gate_b1, L3_cond_gate_w2, L3_cond_gate_b2, L3_cond_resp_w, L3_cond_resp_b)
    return x

_drawn_inputs = setup_inputs


def setup_inputs(seed=0):
    import zlib

    import numpy as np

    out = dict(_drawn_inputs(seed))
    spreads = {'L1_cond_bi': (0.0, 0.377),
     'L1_cond_bo': (0.0, 0.1),
     'L1_cond_gamma': (1.0, 0.2),
     'L1_cond_beta': (0.0, 0.1),
     'L2_cond_ln_gamma': (1.0, 0.2),
     'L2_cond_ln_beta': (0.0, 0.1),
     'L3_cond_safety_bias': (0.0, 0.426),
     'L3_cond_gate_b1': (0.0, 0.8),
     'L3_cond_resp_b': (0.0, 0.472)}
    factors = {'L2_cond_down_b': 6.085,
     'L3_cond_V': 8.0,
     'L3_cond_gate_w1': 4.847,
     'L3_cond_gate_w2': 3.833}
    for name, (base, spread) in spreads.items():
        noise = np.random.default_rng([zlib.crc32(name.encode()), seed]).standard_normal(out[name].shape)
        drawn = base * np.exp(spread * noise) if base else spread * noise
        out[name] = jnp.asarray(drawn.astype(out[name].dtype))
    for name, factor in factors.items():
        out[name] = (out[name] * factor).astype(out[name].dtype)
    return out
```

```python
import concourse.bass as bass
from concourse import mybir
from contextlib import ExitStack


def cond_seq_program(nc, x, expert1_col, expert1_row, expert2_col, expert2_row, angles, safety_tok,
                     l1_wi, l1_wo, l1_rows, down_wt, down_b4, up_t4, up_b, dom_w, dom_b, dom_e,
                     ln_cols, ln_rows, uv, uv_t, gate_w1t, gate_b1, gate_w2, gate_b2, resp_wt,
                     resp_rows, const_f, out):
    f32, bf16, i32 = mybir.dt.float32, mybir.dt.bfloat16, mybir.dt.int32
    ALU, ACT, AX = mybir.AluOpType, mybir.ActivationFunctionType, mybir.AxisListType

    B, S, D = x.shape
    E1 = l1_rows.shape[0]
    IC = l1_wi.shape[2] // D
    A = down_wt.shape[1]
    E2 = dom_b.shape[0]
    R = gate_w1t.shape[1]
    Q = 4
    W = (B + E1 * (Q - 1)) // Q
    NSLOT = W * Q
    NP = 128
    SC = 8
    NX = S // SC
    PS = 3
    NPERM = (S + PS - 1) // PS
    GS0 = 4
    GPQ = 4
    NQ = B * S // (NP * GPQ)
    TQ = NP * GPQ
    TWO_PI_HI, TWO_PI_LO = 6.28125, 0.0019353071795864769
    MAGIC = float(3 * 2 ** 22)
    EPS1, EPS2, EPS3 = 1e-12, 1e-5, 1e-8
    KNOB = min(max(1.0, 0.1), 1.0)

    c_at, c_n = {}, 0
    for name, n in (("ident", NP), ("before", B), ("slots", NSLOT), ("expert", E1), ("part", 1),
                    ("lastrow", A), ("eye32", A), ("before8", E1), ("dummy", NSLOT), ("windows", W), ("one", 1)):
        c_at[name] = (c_n, c_n + n)
        c_n += n

    ctx = ExitStack()
    with ctx:
        def sb(name, shape, dt=f32):
            return ctx.enter_context(nc.sbuf_tensor(name, shape, dt))

        def sem(name):
            return ctx.enter_context(nc.semaphore(name))

        cst = sb("cst", [NP, c_n])

        def const(name, p=NP):
            a, b = c_at[name]
            return cst[0:p, a:b]

        ident = const("ident")
        xb = sb("xb", [B, S, D])
        xr = sb("xr", [B, S, D])
        xT = sb("xT", [D, S, NSLOT])
        bank = sb("bank", [D, E1, 2, IC * D])
        wi_st = sb("wi_st", [D, 2, IC * D])
        wo_st = sb("wo_st", [D, 2, IC * D])
        e1c_i, e2c_i = sb("e1c_i", [B, 1], i32), sb("e2c_i", [B, 1], i32)
        e1r_i, e2r_i = sb("e1r_i", [E1, B], i32), sb("e2r_i", [E2, B], i32)
        e1c, e1r, e2r = sb("e1c", [B, 1]), sb("e1r", [E1, B]), sb("e2r", [E2, B])
        e2f, e2g_i = sb("e2f", [B, 1]), sb("e2g_i", [B, 1], i32)
        oh1 = sb("oh1", [B, E1])
        oh1r = sb("oh1r", [E1, B])
        oh2r = sb("oh2r", [E2, B])
        cnt = sb("cnt", [E1, 4])
        start4 = sb("start4", [E1, 1])
        ohw = sb("ohw", [E1, 2, W])
        rank = sb("rank", [B, 8])
        place = sb("place", [B, NSLOT])
        row_t = sb("row_t", [1, 2, NSLOT])
        dst_i = sb("dst_i", [1, NSLOT], i32)
        ew_i = sb("ew_i", [1, W + 2], i32)
        ang = sb("ang", [B, 12])
        l1r = sb("l1r", [E1, 7 * D])
        parW = sb("parW", [D, 7, W])
        hT = sb("hT", [D, 2, IC * NP])
        rT = sb("rT", [D, 2, NP])
        bst, mv = sb("bst", [NP, 2, 6]), sb("mv", [NP, 2, 2])
        ln_s = sb("ln_s", [NP, 2, 4])
        y1 = sb("y1", [NP, 2, D])
        x1 = sb("x1", [D, B + NSLOT, S])
        mhalf = sb("mhalf", [NP, GPQ])
        phalf, eps1, minus1 = sb("phalf", [NP, 1]), sb("eps1", [NP, 1]), sb("minus1", [NP, 1])
        uv_s, uvt_s = sb("uv_s", [D, 2, A]), sb("uvt_s", [A, 2, D])
        Z, Zp, Zs = sb("Z", [2 * A, 2 * A]), sb("Zp", [2 * A, 2 * A]), sb("Zs", [2 * A, 2 * A])
        gsv = sb("gsv", [2 * A, 8])
        dwt, db4, ut4, upb = sb("dwt", [D, A]), sb("db4", [NP, 1]), sb("ut4", [NP, D]), sb("upb", [D, 1])
        dG = sb("dG", [B, A * A])
        dW = sb("dW", [NP, B // Q, A])
        dbt, det = sb("dbt", [E2, A]), sb("det", [E2, A])
        biasT = sb("biasT", [NP, B // Q])
        xs, ws = sb("xs", [D, 2, TQ]), sb("ws", [NP, 2, GPQ, A])
        hid = sb("hid", [NP, 2, GPQ, S])
        eobd = sb("eobd", [NP, GPQ, Q, S])
        r2 = sb("r2", [D, TQ])
        bst2, mv2 = sb("bst2", [NP, GPQ, 6]), sb("mv2", [NP, 2, GPQ, 2])
        ln2s = sb("ln2s", [NP, 2, 4, GPQ])
        y2 = sb("y2", [NP, 2, TQ])
        lnc, lnr = sb("lnc", [D, 2]), sb("lnr", [NP, 2, D])
        x2T = sb("x2T", [D, 2, TQ])
        x2k = sb("x2k", [NP, 2, TQ])
        tt_s = sb("tt_s", [A, 2, A])
        uo_t, ur, vo = sb("uo_t", [A, D]), sb("ur", [A, A]), sb("vo", [D, A])
        vv, p1, fm = sb("vv", [A, A]), sb("p1", [A, D]), sb("fm", [A, D])
        M = sb("M", [D, D])
        gw1, gb1, gw2, gb2 = sb("gw1", [D, R]), sb("gb1", [R, 1]), sb("gw2", [R, 1]), sb("gb2", [NP, 1])
        rwt, rrow = sb("rwt", [A, D]), sb("rrow", [1, 3, D])
        rsp = sb("rsp", [1, 3, D], bf16)
        rb3, ones3 = sb("rb3", [3, D], bf16), sb("ones3", [3, NP], bf16)
        hb2 = sb("hb2", [NP, 1])
        saf = sb("saf", [NP, 2, B // Q])
        pooled = sb("pooled", [D, 2, GPQ * Q])
        h1 = sb("h1", [R, 2, GPQ * Q])
        stg = sb("stg", [NP, 3, GPQ])
        stt_ = sb("stt_", [NP, 2, GPQ])
        oS = sb("oS", [NP, 2, GPQ, D])

        bk = [ctx.enter_context(nc.psum_tensor(f"bank{i}", [128, 512], f32)) for i in range(8)]

        names = """ld_const ld_ids ld_small ld_wi ld_wo ld_l2 ld_l3 ids_f oh1_done oh1r_done oh2r_done
            cnt_done wcount_a wcount_done start_mm start_done end_done ohw_a ohw_b ohw_done
            rank_mm rank_done base_mm place_done
            row_mm row_a row_b row_c dst_done ew_mm ew_done par_mm par_done
            ang_a ang_b ang_c ang_d ang_e trig_done nst_done rot_a rot_done perm_mm perm_act perm_dve
            wi_staged wo_staged mm1_done gelu_done mm2_done r_done rtok_done bst_done mv_done ve_done
            rstd_done nmean_done nmr_done y1_done y1T_done x1_done
            half_done gram_mm z_done piv_done zs_done gpow_done t0_done gadd_done grec_done t_done
            diag_done dpow_done dadd_done drec_done ts_done post_pe post_cp e2f_a e2f_done e2g_done
            dG_done dwd_done dW_done bias_mm bias_done eobd_zero xs_done ws_done down_done hid_done eo_mm
            eobd_done up_done r2_done u2_done bst2_done mv2_done ve2_done rstd2_done nmean2_done
            nmr2_done y2_done y2T_done x2T_done pool_done x2k_a x2k_done z_done3 h1_mm h1_done st_mm
            tanh_done sig_done st_done o_done out_done rrow_a rsp_a rsp_b rsp_c rsp_d rsp_done
            rb3_done hb2_done saf_a saf_done ones_done""".split()
        s = {n: sem(n) for n in names + [f"ld_x{k}" for k in range(NX)]}

        def after(eng, name, n):
            if not isinstance(n, int) or n > 0:
                eng.wait_ge(s[name], n)

        def ld(eng, dst, src, name):
            eng.dma_start(dst, src).then_inc(s[name], 16)

        dw_dram = nc.dram_tensor("dw_by_batch", (B, A * A), f32, kind="Internal").ap()
        block = ctx.enter_context(nc.Block())
        H = [bk[0], bk[1]]
        OT = [bk[2], bk[3]]
        RK = [bk[4], bk[5]]
        YT = bk[6]

        def run_slots(eng, slot):
            for w in range(4):
                slot(w, w % 2, None)
            with eng.Fori(0, A // 4) as it:
                for j in range(4):
                    slot(it * 4 + (GS0 + j), j % 2, it * 4 + j)
            for w in range(GS0 + A, W + 5):
                slot(w, w % 2, None)

        @block.sync
        def _(sp):
            ld(sp, e1c_i[:, :], expert1_col, "ld_ids")
            ld(sp, e1r_i[:, :], expert1_row.partition_broadcast(E1), "ld_ids")
            ld(sp, cst[:, :], const_f, "ld_const")
            for k in range(NX):
                ld(sp, xb[:, k * SC:(k + 1) * SC, :], x[:, k * SC:(k + 1) * SC, :], f"ld_x{k}")
            ld(sp, bank[:, 0:2, 0, :], l1_wi[0:2].rearrange("e h i -> h e i"), "ld_wi")
            ld(sp, bank[:, 2:E1, 0, :], l1_wi[2:E1].rearrange("e h i -> h e i"), "ld_wi")
            for e in range(E1):
                ld(sp, bank[:, e, 1, :].rearrange("p (c h) -> p c h", c=IC),
                   l1_wo[e].rearrange("(c p) h -> p c h", p=NP), "ld_wo")
            sp.wait_ge(s["dG_done"], 16)
            ld(sp, dw_dram, dG[:, :], "dwd_done")
            sp.wait_ge(s["dwd_done"], 16)
            for q in range(Q):
                ld(sp, dW[A * q:A * q + A, :, :],
                   dw_dram.rearrange("(g q) (a o) -> q a g o", q=Q, a=A)[q], "dW_done")
            for j in range(3):
                if j == 0:
                    sp.wait_ge(s["rsp_done"], 1)
                ld(sp, rb3[j:j + 1, :], rsp[0:1, j, :], "rb3_done")
            for i in range(NQ):
                sp.wait_ge(s["o_done"], i + 1)
                after(sp, "out_done", 16 * i)
                sp.dma_start(out[Q * GPQ * i:Q * GPQ * (i + 1)].rearrange("(g q) s d -> (q s) g d", q=Q),
                             oS[:, i % 2, :, :]).then_inc(s["out_done"], 16)
            sp.wait_ge(s["out_done"], 16 * NQ)

        @block.gpsimd
        def _(pool):
            pool.memset(mhalf[:, :], -0.5)
            pool.memset(phalf[:, :], 0.5)
            pool.memset(eps1[:, :], EPS1)
            pool.memset(minus1[:, :], -1.0)
            pool.memset(ones3[:, :], 1.0).then_inc(s["half_done"], 1)
            pool.memset(eobd[:, :, :, :], 0.0).then_inc(s["eobd_zero"], 1)
            pool.wait_ge(s["half_done"], 1)
            pool.wait_ge(s["e2g_done"], 1)
            pool.indirect_dma_start(dG[:, :], None, dom_w,
                                    bass.IndirectOffsetOnAxis(e2g_i[:, 0:1], 0)).then_inc(s["dG_done"], 16)

            def slot(w, p, j):
                if j is not None:
                    after(pool, "piv_done", j + 1)
                    pool.tensor_tensor(gsv[:, 0:1], Zp[:, bass.ds(j, 1)] if not isinstance(j, int) else Zp[:, j:j + 1],
                                       phalf[0:2 * A, :], ALU.pow).then_inc(s["gpow_done"], 1)
                v = w - 2
                if isinstance(w, int) and not 0 <= v < W:
                    return
                after(pool, "mv_done", v + 1)
                after(pool, "y1_done", v - 1)
                pool.tensor_tensor(ln_s[:, p, 0:1], mv[:, p, 1:2], eps1[:, :], ALU.add).then_inc(s["ve_done"], 1)
                pool.tensor_tensor(ln_s[:, p, 2:3], mv[:, p, 0:1], minus1[:, :], ALU.mult).then_inc(s["nmean_done"], 1)
                after(pool, "ve_done", v + 1)
                pool.tensor_tensor(ln_s[:, p, 1:2], ln_s[:, p, 0:1], mhalf[:, 0:1], ALU.pow).then_inc(s["rstd_done"], 1)
                after(pool, "nmean_done", v + 1)
                after(pool, "rstd_done", v + 1)
                pool.tensor_tensor(ln_s[:, p, 3:4], ln_s[:, p, 2:3], ln_s[:, p, 1:2], ALU.mult).then_inc(s["nmr_done"], 1)

            run_slots(pool, slot)

            pool.wait_ge(s["diag_done"], 1)
            pool.tensor_tensor(gsv[:, 6:7], gsv[:, 5:6], phalf[0:2 * A, :], ALU.pow).then_inc(s["dpow_done"], 1)
            g2 = lnr[:, 0, :].rearrange("p (o d) -> p o d", o=1).broadcast_to([NP, GPQ, D])
            b2 = lnr[:, 1, :].rearrange("p (o d) -> p o d", o=1).broadcast_to([NP, GPQ, D])
            pool.wait_ge(s["ld_l3"], 16 * N_L3)
            for i in range(NQ + 1):
                if i < NQ:
                    p = i % 2
                    pool.wait_ge(s["mv2_done"], i + 1)
                    after(pool, "y2_done", i - 1)
                    pool.tensor_scalar(ln2s[:, p, 0, :], mv2[:, p, :, 1], EPS2, None, ALU.add).then_inc(s["ve2_done"], 1)
                    pool.tensor_scalar(ln2s[:, p, 2, :], mv2[:, p, :, 0], -1.0, None, ALU.mult).then_inc(s["nmean2_done"], 1)
                    pool.wait_ge(s["ve2_done"], i + 1)
                    pool.tensor_tensor(ln2s[:, p, 1, :], ln2s[:, p, 0, :], mhalf[:, :], ALU.pow).then_inc(s["rstd2_done"], 1)
                    pool.wait_ge(s["nmean2_done"], i + 1)
                    pool.wait_ge(s["rstd2_done"], i + 1)
                    pool.tensor_tensor(ln2s[:, p, 3, :], ln2s[:, p, 2, :], ln2s[:, p, 1, :], ALU.mult).then_inc(s["nmr2_done"], 1)
                if i >= 1:
                    k, p = i - 1, (i - 1) % 2
                    pool.wait_ge(s["y2_done"], k + 1)
                    after(pool, "o_done", k - 1)
                    v = x2k[:, p, :].rearrange("p (g d) -> p g d", g=GPQ)
                    pool.tensor_tensor(v, y2[:, p, :].rearrange("p (g d) -> p g d", g=GPQ), g2, ALU.mult).then_inc(s["x2k_a"], 1)
                    pool.wait_ge(s["x2k_a"], k + 1)
                    pool.tensor_tensor(v, v, b2, ALU.add).then_inc(s["x2k_done"], 1)

        quad = xr[:, :, :].rearrange("b s (k r) -> b s k r", r=4)
        quad_in = xb[:, :, :].rearrange("b s (k r) -> b s k r", r=4)

        @block.scalar
        def _(act):
            n = 0
            for dst, src in ((ang[:, 0:2], angles), (e2c_i[:, :], expert2_col),
                             (e2r_i[:, :], expert2_row.partition_broadcast(E2)),
                             (uv_s[:, :, :], uv), (uvt_s[:, :, :], uv_t), (l1r[:, :], l1_rows)):
                ld(act, dst, src, "ld_small")
            for dst, src in ((dwt[:, :], down_wt), (db4[:, :], down_b4), (ut4[:, :], up_t4), (upb[:, :], up_b),
                             (dbt[:, :], dom_b), (det[:, :], dom_e)):
                ld(act, dst, src, "ld_l2")
            act.wait_ge(s["ang_e"], 1)
            act.activation(ang[:, 8:12], ang[:, 4:8], ACT.Sin).then_inc(s["trig_done"], 1)
            act.wait_ge(s["trig_done"], 1)
            for k in range(NX):
                act.wait_ge(s[f"ld_x{k}"], 16)
                r = slice(k * SC, (k + 1) * SC)
                act.activation(quad[:, r, :, 0:2], quad_in[:, r, :, 0:2], ACT.Copy, scale=ang[:, 10:11])
                act.activation(quad[:, r, :, 2:4], quad_in[:, r, :, 2:4], ACT.Copy, scale=ang[:, 11:12])\
                   .then_inc(s["rot_a"], 1)
            for dst, src in ((lnc[:, :], ln_cols), (lnr[:, :, :], ln_rows.partition_broadcast(NP)),
                             (gw1[:, :], gate_w1t), (gb1[:, :], gate_b1), (gw2[:, :], gate_w2),
                             (gb2[:, :], gate_b2.partition_broadcast(NP)), (rwt[:, :], resp_wt),
                             (rrow[:, 0:2, :], resp_rows), (saf[:, 0, :], safety_tok)):
                ld(act, dst, src, "ld_l3")
            for k in range(0, NPERM, 2):
                act.wait_ge(s["perm_mm"], k + 1)
                m = min(PS, S - k * PS)
                act.activation(xT[:, k * PS:k * PS + m, :].rearrange("p s n -> p (s n)"),
                               bk[k % 4][:, 0:m * NSLOT], ACT.Copy).then_inc(s["perm_act"], 1)
            act.wait_ge(s["par_mm"], 1)
            act.activation(parW[:, :, :].rearrange("p c w -> p (c w)"), bk[4][:, 0:7 * W], ACT.Copy)\
               .then_inc(s["par_done"], 1)
            act.wait_ge(s["par_done"], 1)
            act.wait_ge(s["dst_done"], 1)
            regs = [act.alloc_register(f"dst{q}") for q in range(Q)]

            def slot(w, p, j):
                inner = not isinstance(w, int)
                v = w - 4
                if inner or 0 <= v < W:
                    act.load(regs, dst_i[0:1, v * Q:v * Q + Q] if not inner else dst_i[0:1, bass.ds(v * Q, Q)])
                    at = [act.snap(r, min_val=0, max_val=B + NSLOT - 1) for r in regs]
                    after(act, "y1T_done", v + 1)
                    yv = YT[:, 0:NP].rearrange("p (s q) -> p s q", q=Q)
                    for q in range(Q):
                        last = act.activation(x1[:, bass.ds(at[q], 1), :].rearrange("p o s -> p (o s)"), yv[:, :, q],
                                              ACT.Identity, scale=parW[:, 5, bass.ds(v, 1)],
                                              bias=parW[:, 6, bass.ds(v, 1)])
                    last.then_inc(s["x1_done"], 1)
                v = w - 3
                pv = 1 - p
                if inner or 0 <= v < W:
                    after(act, "nmr_done", v + 1)
                    act.activation(y1[:, pv, :], RK[pv][:, 0:D], ACT.Identity, scale=ln_s[:, pv, 1:2],
                                   bias=ln_s[:, pv, 3:4]).then_inc(s["y1_done"], 1)
                if inner or w < W:
                    after(act, "mm2_done", w - 1)
                    after(act, "mm1_done", w + 1)
                    for c in range(IC):
                        act.activation(hT[:, p, c * NP:(c + 1) * NP], H[p][:, c * NP:(c + 1) * NP], ACT.Gelu,
                                       bias=parW[:, c, bass.ds(w, 1)]).then_inc(s["gelu_done"], 1)

            run_slots(act, slot)

            def copies(n, *pairs):
                act.wait_ge(s["post_pe"], n)
                for dst, src in pairs:
                    last = act.activation(dst, src, ACT.Copy)
                last.then_inc(s["post_cp"], 1)
            copies(1, (tt_s[:, :, :].rearrange("k m r -> k (m r)"), bk[7][0:A, 0:2 * A]))
            copies(2, (uo_t[:, :], bk[7][0:A, 0:D]), (ur[:, :], bk[7][0:A, D:D + A]),
                   (vo[:, :], bk[7][:, D + A:D + 2 * A]))
            copies(3, (vv[:, :], bk[7][0:A, 0:A]), (p1[:, :], bk[7][0:A, A:A + D]))
            copies(4, (fm[:, :], bk[7][0:A, 0:D]))
            copies(5, (M[:, :], bk[7][:, 0:D]))
            act.wait_ge(s["ld_l3"], 16 * N_L3)
            act.activation(saf[:, 1, :], saf[:, 0, :], ACT.Tanh, scale=0.5).then_inc(s["saf_a"], 1)
            act.wait_ge(s["hb2_done"], 1)
            act.wait_ge(s["ld_l2"], 16 * 6)

            def gate_h1(k):
                act.wait_ge(s["h1_mm"], k + 1)
                after(act, "st_mm", k - 1)
                act.activation(h1[:, k % 2, :], bk[7][0:R, 0:GPQ * Q], ACT.Relu, bias=gb1[:, :],
                               scale=1.0 / S).then_inc(s["h1_done"], 1)
                act.wait_ge(s["st_mm"], k + 1)
                after(act, "sig_done", k)
                act.activation(stg[:, 0, :], bk[7][:, 64:64 + GPQ], ACT.Tanh, bias=hb2[:, :], scale=0.5)\
                   .then_inc(s["tanh_done"], 1)

            for i in range(NQ + 2):
                if i < NQ:
                    act.wait_ge(s["down_done"], i + 1)
                    after(act, "eo_mm", i - 1)
                    act.activation(hid[:, i % 2, :, :].rearrange("p g s -> p (g s)"), bk[0][:, 0:GPQ * S], ACT.Gelu,
                                   bias=db4[:, :]).then_inc(s["hid_done"], 1)
                if 1 <= i <= NQ:
                    k, p = i - 1, (i - 1) % 2
                    act.wait_ge(s["nmr2_done"], k + 1)
                    after(act, "y2T_done", k - 1)
                    after(act, "x2k_a", k - 1)
                    for g in range(GPQ):
                        last = act.activation(y2[:, p, g * D:(g + 1) * D], bk[3][:, g * D:(g + 1) * D], ACT.Identity,
                                              scale=ln2s[:, p, 1, g:g + 1], bias=ln2s[:, p, 3, g:g + 1])
                    last.then_inc(s["y2_done"], 1)
                    act.wait_ge(s["y2T_done"], k + 1)
                    after(act, "z_done3", k - 1)
                    after(act, "pool_done", k - 1)
                    act.activation(x2T[:, p, :], bk[4][:, :], ACT.Identity, scale=lnc[:, 0:1], bias=lnc[:, 1:2])\
                       .then_inc(s["x2T_done"], 1)
                if i >= 2:
                    gate_h1(i - 2)

        @block.vector
        def _(dve):
            dve.wait_ge(s["ld_ids"], 32)
            dve.tensor_copy(e1c[:, :], e1c_i[:, :])
            dve.tensor_copy(e1r[:, :], e1r_i[:, :]).then_inc(s["ids_f"], 1)
            dve.wait_ge(s["ld_const"], 16)
            dve.wait_ge(s["ids_f"], 1)
            dve.tensor_scalar(oh1r[:, :], e1r[:, :], const("part", E1), None, ALU.is_equal).then_inc(s["oh1r_done"], 1)
            dve.tensor_scalar(oh1[:, :], const("expert"), e1c[:, :], None, ALU.is_equal).then_inc(s["oh1_done"], 1)
            dve.wait_ge(s["oh1r_done"], 1)
            dve.reduce_sum(cnt[:, 0:1], oh1r[:, :], axis=AX.X).then_inc(s["cnt_done"], 1)
            dve.wait_ge(s["cnt_done"], 1)
            dve.tensor_scalar(cnt[:, 3:4], cnt[:, 0:1], 1.0 / Q, (Q - 1) / Q - (Q - 1) / (2 * Q), ALU.mult, ALU.add)\
               .then_inc(s["wcount_a"], 1)
            dve.wait_ge(s["wcount_a"], 1)
            dve.tensor_scalar(cnt[:, 1:2], cnt[:, 3:4], MAGIC, -MAGIC, ALU.add, ALU.add).then_inc(s["wcount_done"], 1)
            dve.wait_ge(s["ld_small"], 16 * 6)
            dve.tensor_scalar(ang[:, 2:4], ang[:, 0:2], 1.0 / (TWO_PI_HI + TWO_PI_LO), MAGIC, ALU.mult, ALU.add)\
               .then_inc(s["ang_a"], 1)
            dve.wait_ge(s["ang_a"], 1)
            dve.tensor_scalar(ang[:, 8:10], ang[:, 2:4], -MAGIC, None, ALU.add).then_inc(s["ang_b"], 1)
            dve.wait_ge(s["ang_b"], 1)
            dve.scalar_tensor_tensor(ang[:, 2:4], ang[:, 8:10], -TWO_PI_HI, ang[:, 0:2], ALU.mult, ALU.add)\
               .then_inc(s["ang_c"], 1)
            dve.wait_ge(s["ang_c"], 1)
            dve.scalar_tensor_tensor(ang[:, 4:6], ang[:, 8:10], -TWO_PI_LO, ang[:, 2:4], ALU.mult, ALU.add)\
               .then_inc(s["ang_d"], 1)
            dve.wait_ge(s["ang_d"], 1)
            dve.scalar_tensor_tensor(ang[:, 2:4], ang[:, 4:6], -1.0, ang[:, 4:6], ALU.mult, ALU.min).then_inc(s["ang_d"], 1)
            dve.wait_ge(s["ang_d"], 2)
            dve.tensor_scalar(ang[:, 6:8], ang[:, 2:4], float(3.14159265358979 / 2), None, ALU.add).then_inc(s["ang_e"], 1)

            dve.wait_ge(s["rank_mm"], 1)
            dve.tensor_tensor_reduce(out=rank[:, 0:E1], in0=bk[5][:, 0:E1], in1=oh1[:, :], scale=1.0, scalar=0.0,
                                     op0=ALU.mult, op1=ALU.add, accum_out=ang[:, 0:1]).then_inc(s["rank_done"], 1)
            dve.wait_ge(s["start_mm"], 1)
            dve.tensor_copy(cnt[:, 2:3], bk[4][0:E1, 500:501])
            dve.tensor_scalar(start4[:, :], bk[4][0:E1, 500:501], float(Q), None, ALU.mult).then_inc(s["start_done"], 1)
            dve.wait_ge(s["start_done"], 1)
            dve.tensor_tensor(cnt[:, 3:4], cnt[:, 2:3], cnt[:, 1:2], ALU.add).then_inc(s["end_done"], 1)
            dve.wait_ge(s["base_mm"], 1)
            dve.wait_ge(s["rank_done"], 1)
            dve.tensor_copy(ang[:, 1:2], bk[6][:, 0:1]).then_inc(s["base_mm"], 1)
            dve.wait_ge(s["base_mm"], 2)
            dve.tensor_scalar(place[:, :], const("slots"), ang[:, 0:1], ang[:, 1:2], ALU.subtract, ALU.is_equal)\
               .then_inc(s["place_done"], 1)
            dve.tensor_scalar(ohw[:, 0, :], const("windows", E1), cnt[:, 2:3], None, ALU.is_ge)
            dve.wait_ge(s["end_done"], 1)
            dve.tensor_scalar(ohw[:, 1, :], const("windows", E1), cnt[:, 3:4], None, ALU.is_lt).then_inc(s["ohw_a"], 1)
            dve.wait_ge(s["ohw_a"], 1)
            dve.tensor_tensor(ohw[:, 0, :], ohw[:, 0, :], ohw[:, 1, :], ALU.mult).then_inc(s["ohw_done"], 1)
            dve.wait_ge(s["trig_done"], 1)
            dve.tensor_scalar(ang[:, 6:8], ang[:, 8:10], -1.0, None, ALU.mult).then_inc(s["nst_done"], 1)
            dve.wait_ge(s["nst_done"], 1)

            def perm_copy(k):
                dve.wait_ge(s["perm_mm"], k + 1)
                m = min(PS, S - k * PS)
                dve.tensor_copy(xT[:, k * PS:k * PS + m, :].rearrange("p s n -> p (s n)"),
                                bk[k % 4][:, 0:m * NSLOT]).then_inc(s["perm_dve"], 1)

            for k in range(NX):
                dve.wait_ge(s["rot_a"], k + 1)
                r = slice(k * SC, (k + 1) * SC)
                for o, i_, c in ((0, 1, 8), (1, 0, 6), (2, 3, 9), (3, 2, 7)):
                    last = dve.scalar_tensor_tensor(quad[:, r, :, o], quad_in[:, r, :, i_], ang[:, c:c + 1],
                                                    quad[:, r, :, o], ALU.mult, ALU.add)
                last.then_inc(s["rot_done"], 1)
                if k == 0:
                    dve.wait_ge(s["row_mm"], 1)
                    dve.tensor_tensor(row_t[:, 0, :], bk[5][0:1, NSLOT:2 * NSLOT], const("dummy", 1), ALU.mult)\
                       .then_inc(s["row_a"], 1)
                    dve.wait_ge(s["row_a"], 1)
                    dve.tensor_tensor(row_t[:, 1, :], const("dummy", 1), row_t[:, 0, :], ALU.subtract)\
                       .then_inc(s["row_b"], 1)
                    dve.wait_ge(s["row_b"], 1)
                    dve.tensor_tensor(dst_i[:, :], row_t[:, 1, :], bk[5][0:1, 0:NSLOT], ALU.add)\
                       .then_inc(s["dst_done"], 1)
                    dve.tensor_copy(ew_i[:, 0:W], bk[5][0:1, 2 * NSLOT:2 * NSLOT + W]).then_inc(s["ew_done"], 1)
            for k in range(1, NPERM, 2):
                perm_copy(k)

            dve.tensor_copy(e2f[:, :], e2c_i[:, :])
            dve.tensor_copy(e2r[:, :], e2r_i[:, :]).then_inc(s["e2f_a"], 1)
            dve.wait_ge(s["e2f_a"], 1)
            dve.tensor_scalar(e2f[:, :], e2f[:, :], 1.0, 0.0, ALU.add, ALU.max)
            dve.tensor_scalar(e2r[:, :], e2r[:, :], 1.0, 0.0, ALU.add, ALU.max).then_inc(s["e2f_done"], 1)
            dve.wait_ge(s["e2f_done"], 1)
            dve.tensor_scalar(e2g_i[:, :], e2f[:, :], float(E2 - 1), None, ALU.min).then_inc(s["e2g_done"], 1)
            dve.tensor_scalar(oh2r[:, :], e2r[:, :], float(E2 - 1), const("part", E2), ALU.min, ALU.is_equal)\
               .then_inc(s["oh2r_done"], 1)
            dve.wait_ge(s["gram_mm"], 1)
            dve.tensor_copy(Z[:, 0:A], bk[7][0:2 * A, 0:A])
            dve.tensor_copy(Z[:, A:2 * A], const("eye32", 2 * A)).then_inc(s["z_done"], 1)
            dve.wait_ge(s["bias_mm"], 1)
            dve.tensor_copy(biasT[:, :], bk[7][:, 64:64 + B // Q]).then_inc(s["bias_done"], 1)
            dve.wait_ge(s["ew_done"], 1)
            ew = dve.alloc_register("ew")

            def stage(w, p, what):
                inner = not isinstance(w, int)
                dve.load([ew], ew_i[0:1, bass.ds(w, 1)] if inner else ew_i[0:1, w:w + 1])
                e = dve.snap(ew, min_val=0, max_val=E1 - 1)
                if what == 0:
                    after(dve, "mm1_done", w - 1)
                    dve.tensor_copy(wi_st[:, p, :], bank[:, bass.ds(e, 1), 0, :].rearrange("p o n -> p (o n)"))\
                       .then_inc(s["wi_staged"], 1)
                else:
                    after(dve, "mm2_done", w - 1)
                    dve.tensor_copy(wo_st[:, p, :], bank[:, bass.ds(e, 1), 1, :].rearrange("p o n -> p (o n)"))\
                       .then_inc(s["wo_staged"], 1)

            swap, rot = [0] * A, [(k + 1) % A for k in range(A)]
            dve.wait_ge(s["ld_wi"], 32)
            stage(0, 0, 0)
            dve.wait_ge(s["ld_wo"], 16 * E1)
            dve.wait_ge(s["par_done"], 1)

            def slot(w, p, j):
                inner = not isinstance(w, int)
                v = w - 2
                if inner:
                    after(dve, "z_done", j + 1)
                if inner or 0 <= v < W:
                    after(dve, "mm2_done", v + 1)
                    after(dve, "rtok_done", v - 1)
                    xv = xT[:, :, bass.ds(v * Q, Q)] if inner else xT[:, :, v * Q:v * Q + Q]
                    dve.scalar_tensor_tensor(rT[:, p, :].rearrange("p (s q) -> p s q", q=Q),
                                             OT[p][:, 0:NP].rearrange("p (s q) -> p s q", q=Q),
                                             parW[:, 4, bass.ds(v, 1)], xv, ALU.add, ALU.add).then_inc(s["r_done"], 1)
                if inner:
                    dve.stream_shuffle(Zp[:, :], Z[:, :], swap).then_inc(s["piv_done"], 1)
                if inner or w + 1 < W:
                    stage(w + 1, 1 - p, 0)
                if inner:
                    dve.stream_shuffle(Zs[:, :], Z[:, :], rot).then_inc(s["zs_done"], 1)
                    after(dve, "zs_done", j + 1)
                    a0 = c_at["lastrow"][0]
                    dve.tensor_tensor(gsv[:, 1:2], Zs[:, bass.ds(j, 1)], cst[0:2 * A, bass.ds(j + a0, 1)], ALU.mult)\
                       .then_inc(s["t0_done"], 1)
                if inner or w < W:
                    stage(w, p, 1)
                if inner:
                    after(dve, "gpow_done", j + 1)
                    dve.tensor_scalar(gsv[:, 2:3], gsv[:, 0:1], EPS3, None, ALU.add).then_inc(s["gadd_done"], 1)
                    after(dve, "gadd_done", j + 1)
                    dve.reciprocal(gsv[:, 3:4], gsv[:, 2:3]).then_inc(s["grec_done"], 1)
                if inner or 0 <= v < W:
                    after(dve, "rtok_done", v + 1)
                    after(dve, "mv_done", v)
                    dve.bn_stats(bst[:, p, :], RK[p][:, 0:D]).then_inc(s["bst_done"], 1)
                    dve.wait_ge(s["par_done"], 1)
                    after(dve, "bst_done", v + 1)
                    after(dve, "nmean_done", v - 1)
                    dve.bn_aggr(mv[:, p, :], bst[:, p, :]).then_inc(s["mv_done"], 1)
                if inner:
                    after(dve, "grec_done", j + 1)
                    after(dve, "t0_done", j + 1)
                    dve.tensor_scalar(gsv[:, 4:5], gsv[:, 1:2], gsv[:, 3:4], gsv[:, 3:4], ALU.mult, ALU.mult)\
                       .then_inc(s["t_done"], 1)
                    after(dve, "t_done", j + 1)
                    dve.scalar_tensor_tensor(Z[:, :], Zp[:, :], gsv[:, 4:5], Zs[:, :], ALU.mult, ALU.add)\
                       .then_inc(s["z_done"], 1)

            run_slots(dve, slot)

            dve.wait_ge(s["z_done"], A + 1)
            dve.tensor_tensor_reduce(out=Zp[:, 0:A], in0=Z[:, 0:A], in1=const("eye32", 2 * A), scale=1.0, scalar=0.0,
                                     op0=ALU.mult, op1=ALU.add, accum_out=gsv[:, 5:6]).then_inc(s["diag_done"], 1)
            dve.wait_ge(s["dpow_done"], 1)
            dve.tensor_scalar(gsv[:, 7:8], gsv[:, 6:7], EPS3, None, ALU.add).then_inc(s["dadd_done"], 1)
            dve.wait_ge(s["dadd_done"], 1)
            dve.reciprocal(gsv[:, 6:7], gsv[:, 7:8]).then_inc(s["drec_done"], 1)
            dve.wait_ge(s["drec_done"], 1)
            dve.tensor_scalar(Zs[:, 0:A], Z[:, A:2 * A], gsv[:, 6:7], None, ALU.mult).then_inc(s["ts_done"], 1)
            dve.wait_ge(s["ld_l3"], 16 * N_L3)
            dve.tensor_tensor(rrow[:, 2, :], rrow[:, 0, :], rrow[:, 1, :], ALU.add).then_inc(s["rrow_a"], 1)
            dve.wait_ge(s["rrow_a"], 1)
            dve.tensor_copy(rsp[:, 0, :], rrow[:, 2, :]).then_inc(s["rsp_a"], 1)
            dve.wait_ge(s["rsp_a"], 1)
            dve.tensor_tensor(rrow[:, 0, :], rrow[:, 2, :], rsp[:, 0, :], ALU.subtract).then_inc(s["rsp_b"], 1)
            dve.wait_ge(s["rsp_b"], 1)
            dve.tensor_copy(rsp[:, 1, :], rrow[:, 0, :]).then_inc(s["rsp_c"], 1)
            dve.wait_ge(s["rsp_c"], 1)
            dve.tensor_tensor(rrow[:, 1, :], rrow[:, 0, :], rsp[:, 1, :], ALU.subtract).then_inc(s["rsp_d"], 1)
            dve.wait_ge(s["rsp_d"], 1)
            dve.tensor_copy(rsp[:, 2, :], rrow[:, 1, :]).then_inc(s["rsp_done"], 1)
            dve.tensor_scalar(hb2[:, :], gb2[:, :], 0.5, None, ALU.mult).then_inc(s["hb2_done"], 1)
            dve.wait_ge(s["saf_a"], 1)
            dve.tensor_scalar(saf[:, 0, :], saf[:, 1, :], 0.5 * KNOB, 0.5 * KNOB, ALU.mult, ALU.add).then_inc(s["saf_done"], 1)
            dve.wait_ge(s["saf_done"], 1)

            def stage2(i):
                p = i % 2
                after(dve, "r2_done", i - 1)
                after(dve, "eo_mm", i - 1)
                dve.tensor_copy(xs[:, p, :], x1[:, Q * GPQ * i:Q * GPQ * (i + 1), :].rearrange("p b s -> p (b s)"))\
                   .then_inc(s["xs_done"], 1)
                dve.tensor_copy(ws[:, p, :, :].rearrange("p g o -> p (g o)"),
                                dW[:, GPQ * i:GPQ * (i + 1), :].rearrange("p g o -> p (g o)")).then_inc(s["ws_done"], 1)

            def pool_sum(k):
                p = k % 2
                dve.wait_ge(s["x2T_done"], k + 1)
                after(dve, "h1_mm", k - 1)
                dve.reduce_sum(pooled[:, p, :], x2T[:, p, :].rearrange("p (b s) -> p b s", s=S), axis=AX.X)\
                   .then_inc(s["pool_done"], 1)

            def finish(k):
                p = k % 2
                dve.wait_ge(s["tanh_done"], k + 1)
                dve.tensor_scalar(stg[:, 1, :], stg[:, 0, :], 0.5, 0.5, ALU.mult, ALU.add).then_inc(s["sig_done"], 1)
                dve.wait_ge(s["sig_done"], k + 1)
                dve.tensor_tensor(stt_[:, p, :], stg[:, 1, :], saf[:, 0, GPQ * k:GPQ * (k + 1)], ALU.mult)\
                   .then_inc(s["st_done"], 1)
                dve.wait_ge(s["st_done"], k + 1)
                dve.wait_ge(s["z_done3"], k + 1)
                dve.wait_ge(s["x2k_done"], k + 1)
                after(dve, "out_done", 16 * (k - 1))
                for g in range(GPQ):
                    last = dve.scalar_tensor_tensor(oS[:, p, g, :], bk[5][:, g * D:(g + 1) * D], stt_[:, p, g:g + 1],
                                                    x2k[:, p, g * D:(g + 1) * D], ALU.mult, ALU.add)
                last.then_inc(s["o_done"], 1)

            dve.wait_ge(s["dW_done"], 16 * Q)
            dve.wait_ge(s["x1_done"], W)
            dve.wait_ge(s["eobd_zero"], 1)
            stage2(0)
            for i in range(NQ + 2):
                if i < NQ:
                    dve.wait_ge(s["eo_mm"], i + 1)
                    after(dve, "up_done", i)
                    for q in range(Q):
                        bb = biasT[A * q:A * q + A, GPQ * i:GPQ * (i + 1)].rearrange("p (g o) -> p g o", o=1)\
                            .broadcast_to([A, GPQ, S])
                        last = dve.tensor_tensor(eobd[A * q:A * q + A, :, q, :],
                                                 bk[1][A * q:A * q + A, 0:GPQ * S].rearrange("p (g s) -> p g s", g=GPQ),
                                                 bb, ALU.add)
                    last.then_inc(s["eobd_done"], 1)
                if i + 1 < NQ:
                    stage2(i + 1)
                if i < NQ:
                    dve.wait_ge(s["up_done"], i + 1)
                    after(dve, "u2_done", i)
                    dve.scalar_tensor_tensor(r2[:, :], bk[2][:, :], upb[:, :], xs[:, i % 2, :], ALU.add, ALU.add)\
                       .then_inc(s["r2_done"], 1)
                if 1 <= i <= NQ:
                    pool_sum(i - 1)
                if i >= 2:
                    finish(i - 2)
                if i < NQ:
                    dve.wait_ge(s["u2_done"], i + 1)
                    for g in range(GPQ):
                        dve.bn_stats(bst2[:, g, :], bk[3][:, g * D:(g + 1) * D]).then_inc(s["bst2_done"], 1)
                    after(dve, "nmean2_done", i - 1)
                    for g in range(GPQ):
                        dve.wait_ge(s["bst2_done"], GPQ * i + g + 1)
                        last = dve.bn_aggr(mv2[:, i % 2, g, :], bst2[:, g, :])
                    last.then_inc(s["mv2_done"], 1)
                    dve.wait_ge(s["mv2_done"], i + 1)

        @block.tensor
        def _(pe):
            mm = pe.matmul
            pe.wait_ge(s["oh1_done"], 1)
            mm(bk[5][:, 0:E1], const("before"), oh1[:, :], start=True, stop=True).then_inc(s["rank_mm"], 1)
            pe.wait_ge(s["wcount_done"], 1)
            mm(bk[4][0:E1, 500:501], const("before8", E1), cnt[:, 1:2], start=True, stop=True).then_inc(s["start_mm"], 1)
            pe.wait_ge(s["start_done"], 1)
            mm(bk[6][:, 0:1], oh1r[:, :], start4[:, :], start=True, stop=True).then_inc(s["base_mm"], 1)
            pe.wait_ge(s["ld_small"], 16 * 6)
            for m in range(2):
                last = mm(bk[7][A * m:A * m + A, 0:A], uv_s[:, m, :], uv_s[:, m, :], start=True, stop=True)
            last.then_inc(s["gram_mm"], 1)
            pe.wait_ge(s["place_done"], 1)
            pe.wait_ge(s["rank_done"], 1)
            mm(bk[5][0:1, 0:NSLOT], const("part"), place[:, :], start=True, stop=True)
            mm(bk[5][0:1, NSLOT:2 * NSLOT], const("one"),
               place[:, :], start=True, stop=True)
            pe.wait_ge(s["ohw_done"], 1)
            mm(bk[5][0:1, 2 * NSLOT:2 * NSLOT + W], const("part", E1), ohw[:, 0, :], start=True, stop=True)\
                .then_inc(s["row_mm"], 1)
            for c in range(7):
                last = mm(bk[4][:, c * W:(c + 1) * W], l1r[:, c * D:(c + 1) * D], ohw[:, 0, :], start=True, stop=True)
            last.then_inc(s["par_mm"], 1)
            for k in range(NPERM):
                for t in range(k * PS, min(S, (k + 1) * PS)):
                    if t % SC == 0:
                        pe.wait_ge(s["rot_done"], t // SC + 1)
                    if t == k * PS and k >= 4:
                        pe.wait_ge(s["perm_act" if k % 2 == 0 else "perm_dve"], k // 2 - 1)
                    last = mm(bk[k % 4][:, (t - k * PS) * NSLOT:(t - k * PS + 1) * NSLOT], xr[:, t, :], place[:, :],
                              start=True, stop=True)
                last.then_inc(s["perm_mm"], 1)
            pe.wait_ge(s["oh2r_done"], 1)
            pe.wait_ge(s["ld_l2"], 16 * 6)
            pe.wait_ge(s["z_done"], 1)
            for q in range(Q):
                mm(bk[7][A * q:A * q + A, 64:64 + B // Q], dbt[:, :], oh2r[:, q:B:Q], start=True, stop=False)
                last = mm(bk[7][A * q:A * q + A, 64:64 + B // Q], det[:, :], oh2r[:, q:B:Q], start=False, stop=True)
            last.then_inc(s["bias_mm"], 1)
            pe.wait_ge(s["perm_act"], (NPERM + 1) // 2)
            pe.wait_ge(s["perm_dve"], NPERM // 2)
            pe.wait_ge(s["par_done"], 1)
            pe.wait_ge(s["ew_done"], 1)

            def slot(w, p, j):
                inner = not isinstance(w, int)
                if inner or w < W:
                    after(pe, "wi_staged", w + 1)
                    after(pe, "gelu_done", (w - 1) * IC)
                    xv = xT[:, :, bass.ds(w * Q, Q)] if inner else xT[:, :, w * Q:w * Q + Q]
                    for c in range(IC):
                        last = mm(H[p][:, c * NP:(c + 1) * NP], wi_st[:, p, c * D:(c + 1) * D], xv, start=True,
                                  stop=True)
                    last.then_inc(s["mm1_done"], 1)
                v = w - 2
                if inner or 0 <= v < W:
                    after(pe, "r_done", v + 1)
                    after(pe, "y1_done", v - 1)
                    pe.transpose(RK[p][:, 0:D], rT[:, p, :], ident).then_inc(s["rtok_done"], 1)
                v, pv = w - 1, 1 - p
                if inner or 0 <= v < W:
                    after(pe, "wo_staged", v + 1)
                    after(pe, "r_done", v - 1)
                    for c in range(IC):
                        after(pe, "gelu_done", v * IC + c + 1)
                        last = mm(OT[pv][:, 0:NP], wo_st[:, pv, c * D:(c + 1) * D], hT[:, pv, c * NP:(c + 1) * NP],
                                  start=(c == 0), stop=(c == IC - 1))
                    last.then_inc(s["mm2_done"], 1)
                v = w - 3
                if inner or 0 <= v < W:
                    after(pe, "y1_done", v + 1)
                    after(pe, "x1_done", v)
                    pe.transpose(YT[:, 0:NP], y1[:, pv, :], ident).then_inc(s["y1T_done"], 1)

            run_slots(pe, slot)

            pe.wait_ge(s["bias_done"], 1)
            pe.wait_ge(s["ts_done"], 1)
            pe.wait_ge(s["ld_l3"], 16 * N_L3)
            pe.transpose(bk[7][0:A, 0:2 * A], Zs[:, 0:A], cst[0:2 * A, 0:2 * A]).then_inc(s["post_pe"], 1)
            pe.wait_ge(s["post_cp"], 1)
            mm(bk[7][0:A, 0:D], tt_s[:, 0, :], uvt_s[:, 0, :], start=True, stop=True)
            mm(bk[7][0:A, D:D + A], uvt_s[:, 0, 0:A], tt_s[:, 0, :], start=True, stop=True)
            mm(bk[7][:, D + A:D + 2 * A], uvt_s[:, 1, :], tt_s[:, 1, :], start=True, stop=True).then_inc(s["post_pe"], 1)
            pe.wait_ge(s["post_cp"], 2)
            mm(bk[7][0:A, 0:A], vo[:, :], vo[:, :], start=True, stop=True)
            mm(bk[7][0:A, A:A + D], ur[:, :], rwt[:, :], start=True, stop=True).then_inc(s["post_pe"], 1)
            pe.wait_ge(s["post_cp"], 3)
            mm(bk[7][0:A, 0:D], vv[:, :], p1[:, :], start=True, stop=True).then_inc(s["post_pe"], 1)
            pe.wait_ge(s["post_cp"], 4)
            mm(bk[7][:, 0:D], uo_t[:, :], fm[:, :], start=True, stop=True).then_inc(s["post_pe"], 1)
            pe.wait_ge(s["post_cp"], 5)

            def down(i):
                pe.wait_ge(s["xs_done"], i + 1)
                after(pe, "hid_done", i)
                v = xs[:, i % 2, :].rearrange("p (g q s) -> p g q s", g=GPQ, q=Q)
                for q in range(Q):
                    last = mm(bk[0][A * q:A * q + A, 0:GPQ * S], dwt[:, :], v[:, :, q, :], start=True, stop=True)
                last.then_inc(s["down_done"], 1)

            def expert(i):
                pe.wait_ge(s["hid_done"], i + 1)
                pe.wait_ge(s["ws_done"], i + 1)
                after(pe, "eobd_done", i)
                for g in range(GPQ):
                    for q in range(Q):
                        r = slice(A * q, A * q + A)
                        last = mm(bk[1][r, g * S:(g + 1) * S], ws[r, i % 2, g, :], hid[r, i % 2, g, :],
                                  start=True, stop=True)
                last.then_inc(s["eo_mm"], 1)

            def up(i):
                pe.wait_ge(s["eobd_done"], i + 1)
                after(pe, "r2_done", i)
                mm(bk[2][:, :], ut4[:, :], eobd[:, :, :, :].rearrange("p g q s -> p (g q s)"), start=True, stop=True)\
                    .then_inc(s["up_done"], 1)

            def to_tokens(i):
                pe.wait_ge(s["r2_done"], i + 1)
                after(pe, "y2_done", i)
                for g in range(GPQ):
                    last = pe.transpose(bk[3][:, g * D:(g + 1) * D], r2[:, g * D:(g + 1) * D], ident)
                last.then_inc(s["u2_done"], 1)

            def back(i):
                pe.wait_ge(s["y2_done"], i + 1)
                after(pe, "x2T_done", i)
                for g in range(GPQ):
                    last = pe.transpose(bk[4][:, g * D:(g + 1) * D], y2[:, i % 2, g * D:(g + 1) * D], ident)
                last.then_inc(s["y2T_done"], 1)

            def response(i):
                pe.wait_ge(s["pool_done"], i + 1)
                after(pe, "tanh_done", i)
                mm(bk[7][0:R, 0:GPQ * Q], gw1[:, :], pooled[:, i % 2, :], start=True, stop=True).then_inc(s["h1_mm"], 1)
                after(pe, "o_done", i)
                mm(bk[5][:, :], ones3[:, :], rb3[:, :].rearrange("k (o d) -> k o d", o=1).broadcast_to([3, GPQ, D]),
                   start=True, stop=False)
                for g in range(GPQ):
                    last = mm(bk[5][:, g * D:(g + 1) * D], x2T[:, i % 2, g * D:(g + 1) * D], M[:, :], start=False,
                              stop=(g == GPQ - 1))
                last.then_inc(s["z_done3"], 1)

            def strength(i):
                pe.wait_ge(s["h1_done"], i + 1)
                for q in range(Q):
                    last = mm(bk[7][S * q:S * q + S, 64:64 + GPQ], gw2[:, 0:1].broadcast_to([R, S]),
                              h1[:, i % 2, q:GPQ * Q:Q], start=True, stop=True)
                last.then_inc(s["st_mm"], 1)

            pe.wait_ge(s["rb3_done"], 48)
            pe.wait_ge(s["half_done"], 1)
            down(0)
            for i in range(NQ + 2):
                if i < NQ:
                    expert(i)
                if i + 1 < NQ:
                    down(i + 1)
                if i < NQ:
                    up(i)
                if 1 <= i <= NQ:
                    back(i - 1)
                if i >= 2:
                    response(i - 2)
                if i < NQ:
                    to_tokens(i)
                if i >= 2:
                    strength(i - 2)


N_L3 = 9


def kernel(**inputs):
    import numpy as np
    import concourse.bacc as bacc
    from concourse import mybir
    from concourse.bass_utils import run_bass_kernel_spmd

    a = {k: np.asarray(v) for k, v in inputs.items()}
    f = np.float32
    B, S, D = a["x"].shape
    E1, E2 = a["L1_cond_Wi"].shape[0], a["L2_cond_expert_W"].shape[0]
    A = a["L2_cond_down_W"].shape[0]
    Q = 4
    W = (B + E1 * (Q - 1)) // Q
    NSLOT = W * Q
    p = np.arange(128)
    lastrow = np.where((p[:, None] % A) <= A - 2 - np.arange(A)[None], -1.0, 0.0)
    const = np.concatenate([
        np.eye(128), (p[:, None] < p[None, :]), np.tile(np.arange(NSLOT), (128, 1)), np.tile(np.arange(E1), (128, 1)),
        p[:, None], lastrow, np.eye(A)[p % A], (p[:, None] < np.arange(E1)[None]),
        np.tile(np.arange(NSLOT) + B, (128, 1)), np.tile(np.arange(W), (128, 1)), np.ones((128, 1))], axis=1).astype(f)
    eye = np.eye(A, dtype=f).reshape(1, A * A)
    wt = a["L2_cond_expert_W"].transpose(0, 2, 1).reshape(E2, A * A)
    zero = np.zeros((1, A), f)
    emb = a["L2_cond_domain_emb"]
    l1_rows = np.concatenate([a["L1_cond_bi"], a["L1_cond_bo"], a["L1_cond_gamma"], a["L1_cond_beta"]], axis=1)
    ins = {
        "x": a["x"],
        "expert1_col": a["itok_B_0_7"].reshape(B, 1), "expert1_row": a["itok_B_0_7"],
        "expert2_col": a["itok_B_0_15"].reshape(B, 1), "expert2_row": a["itok_B_0_15"],
        "angles": np.stack([a["condB_theta"], a["condB_phi"]], axis=1),
        "safety_tok": np.repeat(a["condB_safetyscore"].reshape(B // Q, Q).T, S, axis=0),
        "l1_wi": a["L1_cond_Wi"], "l1_wo": a["L1_cond_Wo"], "l1_rows": l1_rows,
        "down_wt": a["L2_cond_down_W"].T, "down_b4": np.tile(a["L2_cond_down_b"], Q).reshape(Q * A, 1),
        "up_t4": np.tile(a["L2_cond_up_W"].T, (Q, 1)), "up_b": a["L2_cond_up_b"].reshape(D, 1),
        "dom_w": np.concatenate([eye, wt, eye]),
        "dom_b": np.concatenate([zero, a["L2_cond_expert_b"], zero]),
        "dom_e": np.concatenate([emb[:1], emb, emb[-1:]]),
        "ln_cols": np.stack([a["L2_cond_ln_gamma"], a["L2_cond_ln_beta"]], axis=1),
        "ln_rows": np.stack([a["L2_cond_ln_gamma"], a["L2_cond_ln_beta"]]),
        "uv": np.stack([a["L3_cond_U"], a["L3_cond_V"]], axis=1),
        "uv_t": np.stack([a["L3_cond_U"].T, a["L3_cond_V"].T], axis=1),
        "gate_w1t": a["L3_cond_gate_w1"].T, "gate_b1": a["L3_cond_gate_b1"].reshape(-1, 1),
        "gate_w2": a["L3_cond_gate_w2"].reshape(-1, 1), "gate_b2": a["L3_cond_gate_b2"],
        "resp_wt": a["L3_cond_resp_w"].T,
        "resp_rows": np.stack([a["L3_cond_resp_b"], a["L3_cond_safety_bias"]]).reshape(1, 2, D),
        "const_f": const,
    }
    nc = bacc.Bacc("TRN2", target_bir_lowering=False, num_devices=1)
    arrays, args = {}, {}
    for name, v in ins.items():
        v = np.ascontiguousarray(v)
        arrays[f"in_{name}"] = v
        args[name] = nc.dram_tensor(f"in_{name}", v.shape, mybir.dt.from_np(v.dtype), kind="ExternalInput").ap()
    out = nc.dram_tensor("out_0", (B, S, D), mybir.dt.float32, kind="ExternalOutput").ap()
    cond_seq_program(nc, out=out, **args)
    r = run_bass_kernel_spmd(nc, [arrays], core_ids=[0])
    return r.results[0]["out_0"]
```

```python
import concourse.bass as bass
from concourse import mybir
from contextlib import ExitStack


def cond_seq_program(nc, x, expert1_col, expert1_row, expert2_col, expert2_row, angles, safety_tok,
                     l1_wi, l1_wo, l1_bi, l1_vec, down_wt, down_b4, up_t4, up_b, dom_w, dom_b, dom_e,
                     ln_cols, ln_rows, uv, uv_t, gate_w1t, gate_b1, gate_w2, gate_b2, resp_wt,
                     resp_rows, const_f, out):
    f32, bf16, i32 = mybir.dt.float32, mybir.dt.bfloat16, mybir.dt.int32
    ALU, ACT, AX = mybir.AluOpType, mybir.ActivationFunctionType, mybir.AxisListType

    B, S, D = x.shape
    E1 = l1_bi.shape[0]
    IC = l1_wi.shape[2] // D
    A = down_wt.shape[1]
    E2 = dom_b.shape[0]
    R = gate_w1t.shape[1]
    Q = 4
    W = (B + E1 * (Q - 1)) // Q
    NSLOT = W * Q
    WP = -(-W // 4) * 4
    NP = 128
    SC = 8
    NX = S // SC
    PS = 3
    NPERM = (S + PS - 1) // PS
    NY = 4
    GPQ = 4
    NQ = B * S // (NP * GPQ)
    TQ = NP * GPQ
    TWO_PI_HI, TWO_PI_LO = 6.28125, 0.0019353071795864769
    MAGIC = float(3 * 2 ** 22)
    EPS1, EPS2, EPS3 = 1e-12, 1e-5, 1e-8
    KNOB = min(max(1.0, 0.1), 1.0)

    c_at, c_n = {}, 0
    for name, n in (("ident", NP), ("before", B), ("slots", NSLOT), ("expert", E1), ("part", 1), ("lastrow", A),
                    ("eye32", A), ("before8", E1), ("windows", WP), ("rowmat", Q * NP), ("rowbase", W), ("fromend", 1)):
        c_at[name] = (c_n, c_n + n)
        c_n += n

    ctx = ExitStack()
    with ctx:
        def sb(name, shape, dt=f32):
            return ctx.enter_context(nc.sbuf_tensor(name, shape, dt))

        def sem(name):
            return ctx.enter_context(nc.semaphore(name))

        cst = sb("cst", [NP, c_n])

        def const(name, p=NP):
            a, b = c_at[name]
            return cst[0:p, a:b]

        ident = const("ident")
        xb = sb("xb", [B, S, D])
        xr = sb("xr", [B, S, D])
        xT = sb("xT", [D, W, S, Q])
        bank = sb("bank", [D, E1, 2, IC * D])
        vec = sb("vec", [NP, E1, 3, D])
        wi_st = sb("wi_st", [D, 2, IC * D])
        e1c_i, e2c_i = sb("e1c_i", [B, 1], i32), sb("e2c_i", [B, 1], i32)
        e1r_i, e2r_i = sb("e1r_i", [E1, B], i32), sb("e2r_i", [E2, B], i32)
        e1c, e1r, e2r = sb("e1c", [B, 1]), sb("e1r", [E1, B]), sb("e2r", [E2, B])
        e2f, e2g_i = sb("e2f", [B, 1]), sb("e2g_i", [B, 1], i32)
        oh1 = sb("oh1", [B, E1])
        oh1r = sb("oh1r", [E1, B])
        oh2r = sb("oh2r", [E2, B])
        cnt = sb("cnt", [E1, 4])
        start4 = sb("start4", [E1, 1])
        ohw = sb("ohw", [E1, 2, WP])
        rank = sb("rank", [B, 8])
        placed = sb("placed", [B, NSLOT])
        place = sb("place", [B, NSLOT])
        row_i = sb("row_i", [NP, W], i32)
        ew_i = sb("ew_i", [1, WP], i32)
        ang = sb("ang", [B, 12])
        bi_s = sb("bi_s", [E1, IC * D])
        biW = sb("biW", [D, IC, W])
        hT = sb("hT", [D, 2, IC * NP])
        r1 = sb("r1", [NP, 2, D])
        bst, mv = sb("bst", [NP, 6]), sb("mv", [NP, 2, 2])
        ve, rstd = sb("ve", [NP, 2]), sb("rstd", [NP, 2])
        yg = sb("yg", [NP, D])
        y1 = sb("y1", [NP, NY, D])
        mhalf = sb("mhalf", [NP, GPQ])
        phalf = sb("phalf", [NP, 1])
        uv_s, uvt_s = sb("uv_s", [D, 2, A]), sb("uvt_s", [A, 2, D])
        Z, Zp, Zs = sb("Z", [2 * A, 2 * A]), sb("Zp", [2 * A, 2 * A]), sb("Zs", [2 * A, 2 * A])
        gsv = sb("gsv", [2 * A, 8])
        dwt, db4, ut4 = sb("dwt", [D, A]), sb("db4", [NP, 1]), sb("ut4", [NP, D])
        dG = sb("dG", [B, A * A])
        dW = sb("dW", [NP, B // Q, Q, A])
        dbt, det = sb("dbt", [E2, A]), sb("det", [E2, A])
        biasT = sb("biasT", [NP, B // Q])
        x1k = xb[:, :, :].rearrange("p s d -> p (s d)").rearrange("p (i n) -> p i n", i=NQ)
        x1T = sb("x1T", [D, 2, TQ])
        hid = sb("hid", [NP, 2, GPQ * S])
        eobd = sb("eobd", [NP, GPQ, Q, S])
        r2 = sb("r2", [NP, 2, TQ])
        bst2, mv2 = sb("bst2", [NP, GPQ, 6]), sb("mv2", [NP, 2, GPQ, 2])
        ln2s = sb("ln2s", [NP, 2, 4, GPQ])
        y2 = sb("y2", [NP, 2, TQ])
        lnc, lnr = sb("lnc", [D, 2]), sb("lnr", [NP, 2, D])
        x2T = sb("x2T", [D, 2, TQ])
        x2k = sb("x2k", [NP, 2, TQ])
        tt_s = sb("tt_s", [A, 2, A])
        uo_t, ur, vo = sb("uo_t", [A, D]), sb("ur", [A, A]), sb("vo", [D, A])
        vv, p1, fm = sb("vv", [A, A]), sb("p1", [A, D]), sb("fm", [A, D])
        M = sb("M", [D, D])
        gw1, gb1, gw2, gb2 = sb("gw1", [D, R]), sb("gb1", [R, 1]), sb("gw2", [R, 1]), sb("gb2", [NP, 1])
        rwt, rrow = sb("rwt", [A, D]), sb("rrow", [1, 4, D])
        rsp = sb("rsp", [1, 2, 3, D], bf16)
        rb3, ones3 = sb("rb3", [3, 2, D], bf16), sb("ones3", [3, NP], bf16)
        hb2 = sb("hb2", [NP, 1])
        saf = sb("saf", [NP, 2, B // Q])
        pooled = sb("pooled", [D, 2, GPQ * Q])
        h1 = sb("h1", [R, 2, GPQ * Q])
        stg = sb("stg", [NP, 3, GPQ])
        stt_ = sb("stt_", [NP, 2, GPQ])
        oS = sb("oS", [NP, 2, GPQ, D])

        bk = [ctx.enter_context(nc.psum_tensor(f"bank{i}", [128, 512], f32)) for i in range(8)]

        names = """ld_const ld_ids ld_small ld_wi ld_wo ld_vec ld_l2 ld_l3 ids_f oh1_done oh1r_done oh2r_done
            cnt_done wcount_a wcount_done start_mm start_done end_done ohw_a ohw_done rank_mm rank_done
            base_mm base_done place_done placed_done ew_mm ew_done row_mm row_done bi_mm bi_done
            ang_a ang_b ang_c ang_d ang_e trig_done nst_done rot_a rot_done perm_mm perm_act perm_dve
            wi_staged mm1_done gelu_done mm2_done r_done bst_done mv_done ve_done rstd_done yg_done y1_done
            half_done gram_mm z_done piv_done zs_done gpow_done t0_done gadd_done grec_done t_done
            diag_done dpow_done dadd_done drec_done ts_done post_pe post_cp e2f_a e2f_done e2g_done
            dG_done dwd_done dW_zero dW_done bias_mm bias_done eobd_zero xp_done x1T_done down_done hid_done
            eo_mm eobd_done up_done r2_done bst2_done mv2_done ve2_done rstd2_done nmean2_done
            nmr2_done y2_done y2T_done x2T_done pool_done x2k_a x2k_done z_done3 h1_mm h1_done st_mm
            tanh_done sig_done st_done o_done out_done rrow_a rsp_a rsp_b rsp_c rsp_d rsp_done
            rb3_done hb2_done saf_a saf_done""".split()
        s = {n: sem(n) for n in names + [f"ld_x{k}" for k in range(NX)]
             + [f"ld_x1_{k}" for k in range(NQ)] + [f"y1_stored_{k}" for k in range(NY)]}

        def after(eng, name, n):
            if not isinstance(n, int) or n > 0:
                eng.wait_ge(s[name], n)

        def ld(eng, dst, src, name):
            eng.dma_start(dst, src).then_inc(s[name], 16)

        x1_dram = nc.dram_tensor("layer1_out", ((B + NSLOT) * S, D), f32, kind="Internal").ap()
        dw_dram = nc.dram_tensor("dw_by_batch", (B, A * A), f32, kind="Internal").ap()
        block = ctx.enter_context(nc.Block())
        H = [[bk[0], bk[1]], [bk[2], bk[3]]]
        OT = [bk[4], bk[5]]

        def expert_regs(eng, name):
            regs = [[eng.alloc_register(f"{name}{k}{j}") for j in range(4)] for k in range(2)]

            def load(w):
                if w % 4 == 0:
                    eng.load(regs[w // 4 % 2], ew_i[0:1, w:w + 4])

            def at(w):
                return eng.snap(regs[w // 4 % 2][w % 4], min_val=0, max_val=E1 - 1)
            return load, at

        SLOTS = W + 4
        POST = A + 2

        @block.sync
        def _(sp):
            ld(sp, e1c_i[:, :], expert1_col, "ld_ids")
            ld(sp, e1r_i[:, :], expert1_row.partition_broadcast(E1), "ld_ids")
            ld(sp, cst[:, :], const_f, "ld_const")
            for k in range(NX):
                ld(sp, xb[:, k * SC:(k + 1) * SC, :], x[:, k * SC:(k + 1) * SC, :], f"ld_x{k}")
            ld(sp, bank[:, 0:2, 0, :], l1_wi[0:2].rearrange("e h i -> h e i"), "ld_wi")
            ld(sp, bank[:, 2:E1, 0, :], l1_wi[2:E1].rearrange("e h i -> h e i"), "ld_wi")
            ld(sp, vec[:, :, :, :], l1_vec.partition_broadcast(NP), "ld_vec")
            for e in range(E1):
                ld(sp, bank[:, e, 1, :].rearrange("p (c h) -> p c h", c=IC),
                   l1_wo[e].rearrange("(c p) h -> p c h", p=NP), "ld_wo")
            sp.wait_ge(s["dG_done"], 16)
            ld(sp, dw_dram, dG[:, :], "dwd_done")
            sp.wait_ge(s["dwd_done"], 16)
            sp.wait_ge(s["dW_zero"], 1)
            for q in range(Q):
                ld(sp, dW[A * q:A * q + A, :, q, :],
                   dw_dram.rearrange("(g q) (a o) -> q a g o", q=Q, a=A)[q], "dW_done")
            sp.wait_ge(s["rsp_done"], 2)
            for k in range(2):
                for j in range(3):
                    ld(sp, rb3[j:j + 1, k, :], rsp[0:1, k, j, :], "rb3_done")
            for k in range(NY):
                sp.wait_ge(s[f"y1_stored_{k}"], 16 * len(range(k, W, NY)))
            for i in range(NQ):
                ld(sp, x1k[:, i, :].rearrange("p (g d) -> p g d", g=GPQ),
                   x1_dram[TQ * i:TQ * (i + 1)].rearrange("(g p) d -> p g d", p=NP), f"ld_x1_{i}")
            for i in range(NQ):
                sp.wait_ge(s["o_done"], i + 1)
                after(sp, "out_done", 16 * i)
                sp.dma_start(out[Q * GPQ * i:Q * GPQ * (i + 1)].rearrange("(g q) s d -> (q s) g d", q=Q),
                             oS[:, i % 2, :, :]).then_inc(s["out_done"], 16)
            sp.wait_ge(s["out_done"], 16 * NQ)

        @block.gpsimd
        def _(pool):
            pool.memset(mhalf[:, :], -0.5)
            pool.memset(phalf[:, :], 0.5)
            pool.memset(ones3[:, :], 1.0).then_inc(s["half_done"], 1)
            pool.memset(eobd[:, :, :, :], 0.0).then_inc(s["eobd_zero"], 1)
            pool.memset(dW[:, :, :, :], 0.0).then_inc(s["dW_zero"], 1)
            pool.wait_ge(s["half_done"], 1)
            pool.wait_ge(s["e2g_done"], 1)
            pool.indirect_dma_start(dG[:, :], None, dom_w,
                                    bass.IndirectOffsetOnAxis(e2g_i[:, 0:1], 0)).then_inc(s["dG_done"], 16)

            pool.wait_ge(s["row_done"], 1)
            for w in range(SLOTS):
                if w < A:
                    pool.wait_ge(s["piv_done"], w + 1)
                    pool.tensor_tensor(gsv[:, 0:1], Zp[:, w:w + 1], phalf[0:2 * A, :], ALU.pow)\
                        .then_inc(s["gpow_done"], 1)
                v = w - 2
                if 0 <= v < W:
                    p = v % 2
                    pool.wait_ge(s["mv_done"], v + 1)
                    after(pool, "y1_done", v - 1)
                    pool.tensor_scalar(ve[:, p:p + 1], mv[:, p, 1:2], EPS1, None, ALU.add).then_inc(s["ve_done"], 1)
                    pool.wait_ge(s["ve_done"], v + 1)
                    pool.tensor_tensor(rstd[:, p:p + 1], ve[:, p:p + 1], mhalf[:, 0:1], ALU.pow)\
                        .then_inc(s["rstd_done"], 1)
                v = w - 3
                if 0 <= v < W:
                    pool.wait_ge(s["y1_done"], v + 1)
                    pool.indirect_dma_start(x1_dram, bass.IndirectOffsetOnAxis(row_i[:, v:v + 1], 0),
                                            y1[:, v % NY, :], None).then_inc(s[f"y1_stored_{v % NY}"], 16)
                if w == POST - 1:
                    pool.wait_ge(s["diag_done"], 1)
                    pool.tensor_tensor(gsv[:, 6:7], gsv[:, 5:6], phalf[0:2 * A, :], ALU.pow).then_inc(s["dpow_done"], 1)

            g2 = lnr[:, 0, :].rearrange("p (o d) -> p o d", o=1).broadcast_to([NP, GPQ, D])
            b2 = lnr[:, 1, :].rearrange("p (o d) -> p o d", o=1).broadcast_to([NP, GPQ, D])
            pool.wait_ge(s["ld_l3"], 16 * N_L3)
            for i in range(NQ + 1):
                if i < NQ:
                    p = i % 2
                    pool.wait_ge(s["mv2_done"], i + 1)
                    after(pool, "y2_done", i - 1)
                    pool.tensor_scalar(ln2s[:, p, 0, :], mv2[:, p, :, 1], EPS2, None, ALU.add).then_inc(s["ve2_done"], 1)
                    pool.tensor_scalar(ln2s[:, p, 2, :], mv2[:, p, :, 0], -1.0, None, ALU.mult).then_inc(s["nmean2_done"], 1)
                    pool.wait_ge(s["ve2_done"], i + 1)
                    pool.tensor_tensor(ln2s[:, p, 1, :], ln2s[:, p, 0, :], mhalf[:, :], ALU.pow).then_inc(s["rstd2_done"], 1)
                    pool.wait_ge(s["nmean2_done"], i + 1)
                    pool.wait_ge(s["rstd2_done"], i + 1)
                    pool.tensor_tensor(ln2s[:, p, 3, :], ln2s[:, p, 2, :], ln2s[:, p, 1, :], ALU.mult).then_inc(s["nmr2_done"], 1)
                if i >= 1:
                    k, p = i - 1, (i - 1) % 2
                    pool.wait_ge(s["y2_done"], k + 1)
                    after(pool, "o_done", k - 1)
                    v = x2k[:, p, :].rearrange("p (g d) -> p g d", g=GPQ)
                    pool.tensor_tensor(v, y2[:, p, :].rearrange("p (g d) -> p g d", g=GPQ), g2, ALU.mult).then_inc(s["x2k_a"], 1)
                    pool.wait_ge(s["x2k_a"], k + 1)
                    pool.tensor_tensor(v, v, b2, ALU.add).then_inc(s["x2k_done"], 1)

        quad = xr[:, :, :].rearrange("b s (k r) -> b s k r", r=4)
        quad_in = xb[:, :, :].rearrange("b s (k r) -> b s k r", r=4)

        @block.scalar
        def _(act):
            n = 0
            for dst, src in ((ang[:, 0:2], angles), (e2c_i[:, :], expert2_col),
                             (e2r_i[:, :], expert2_row.partition_broadcast(E2)),
                             (uv_s[:, :, :], uv), (uvt_s[:, :, :], uv_t), (bi_s[:, :], l1_bi)):
                ld(act, dst, src, "ld_small")
            for dst, src in ((dwt[:, :], down_wt), (db4[:, :], down_b4), (ut4[:, :], up_t4),
                             (dbt[:, :], dom_b), (det[:, :], dom_e)):
                ld(act, dst, src, "ld_l2")
            act.wait_ge(s["ang_e"], 1)
            act.activation(ang[:, 8:12], ang[:, 4:8], ACT.Sin).then_inc(s["trig_done"], 1)
            act.wait_ge(s["trig_done"], 1)
            for k in range(NX):
                act.wait_ge(s[f"ld_x{k}"], 16)
                r = slice(k * SC, (k + 1) * SC)
                act.activation(quad[:, r, :, 0:2], quad_in[:, r, :, 0:2], ACT.Copy, scale=ang[:, 10:11])
                act.activation(quad[:, r, :, 2:4], quad_in[:, r, :, 2:4], ACT.Copy, scale=ang[:, 11:12])\
                   .then_inc(s["rot_a"], 1)
            for dst, src in ((lnc[:, :], ln_cols), (lnr[:, :, :], ln_rows.partition_broadcast(NP)),
                             (gw1[:, :], gate_w1t), (gb1[:, :], gate_b1), (gw2[:, :], gate_w2),
                             (gb2[:, :], gate_b2.partition_broadcast(NP)), (rwt[:, :], resp_wt),
                             (rrow[:, 0:2, :], resp_rows), (rrow[:, 2:3, :], up_b), (saf[:, 0, :], safety_tok)):
                ld(act, dst, src, "ld_l3")
            for k in range(0, NPERM, 2):
                act.wait_ge(s["perm_mm"], k + 1)
                m = min(PS, S - k * PS)
                act.activation(xT[:, :, k * PS:k * PS + m, :],
                               bk[k % 4][:, 0:m * NSLOT].rearrange("p (s w q) -> p w s q", s=m, q=Q), ACT.Copy).then_inc(s["perm_act"], 1)
            act.wait_ge(s["bi_mm"], 1)
            act.activation(biW[:, :, :].rearrange("p c w -> p (c w)"), bk[4][:, 0:IC * W], ACT.Copy)\
               .then_inc(s["bi_done"], 1)
            act.wait_ge(s["ew_done"], 1)
            act_load, act_expert = expert_regs(act, "act")

            def stage(w):
                act_load(w)
                e = act_expert(w)
                after(act, "mm1_done", 2 * (w - 1))
                act.activation(wi_st[:, w % 2, :], bank[:, bass.ds(e, 1), 0, :].rearrange("p o n -> p (o n)"), ACT.Copy)\
                   .then_inc(s["wi_staged"], 1)

            def copies(n):
                act.wait_ge(s["post_pe"], n)
                for dst, src in (((tt_s[:, :, :].rearrange("k m r -> k (m r)"), bk[7][0:A, 0:2 * A]),),
                                 ((uo_t[:, :], bk[7][0:A, 0:D]), (ur[:, :], bk[7][0:A, D:D + A]),
                                  (vo[:, :], bk[7][:, D + A:D + 2 * A])),
                                 ((vv[:, :], bk[7][0:A, 0:A]), (p1[:, :], bk[7][0:A, A:A + D])),
                                 ((fm[:, :], bk[7][0:A, 0:D]),),
                                 ((M[:, :], bk[7][:, 0:D]),))[n - 1]:
                    last = act.activation(dst, src, ACT.Copy)
                last.then_inc(s["post_cp"], 1)

            act.wait_ge(s["ld_wi"], 32)
            stage(0)
            act.wait_ge(s["bi_done"], 1)
            for w in range(SLOTS):
                if w + 1 < W:
                    stage(w + 1)
                if w < W:
                    after(act, "mm2_done", w - 1)
                    for c in range(IC):
                        if c % 2 == 0:
                            act.wait_ge(s["mm1_done"], 2 * w + c // 2 + 1)
                        act.activation(hT[:, w % 2, c * NP:(c + 1) * NP], H[w % 2][c // 2][:, (c % 2) * NP:(c % 2 + 1) * NP],
                                       ACT.Gelu, bias=biW[:, c, w:w + 1]).then_inc(s["gelu_done"], 1)
                if POST < w <= POST + 5:
                    copies(w - POST)
                if w == POST + 6:
                    act.wait_ge(s["ld_l3"], 16 * N_L3)
                    act.activation(saf[:, 1, :], saf[:, 0, :], ACT.Tanh, scale=0.5).then_inc(s["saf_a"], 1)
            act.wait_ge(s["hb2_done"], 1)
            act.wait_ge(s["ld_l2"], 16 * 5)

            def gate_h1(k):
                act.wait_ge(s["h1_mm"], k + 1)
                after(act, "st_mm", k - 1)
                act.activation(h1[:, k % 2, :], bk[7][0:R, 0:GPQ * Q], ACT.Relu, bias=gb1[:, :],
                               scale=1.0 / S).then_inc(s["h1_done"], 1)
                act.wait_ge(s["st_mm"], k + 1)
                after(act, "sig_done", k)
                act.activation(stg[:, 0, :], bk[7][:, 64:64 + GPQ], ACT.Tanh, bias=hb2[:, :], scale=0.5)\
                   .then_inc(s["tanh_done"], 1)

            def x1_T(i):
                act.wait_ge(s["xp_done"], i + 1)
                after(act, "down_done", i - 1)
                act.activation(x1T[:, i % 2, :], bk[6][:, :], ACT.Copy).then_inc(s["x1T_done"], 1)

            def hidden(i):
                act.wait_ge(s["down_done"], i + 1)
                after(act, "eo_mm", i - 1)
                act.activation(hid[:, i % 2, :], bk[0][:, 0:GPQ * S], ACT.Gelu, bias=db4[:, :]).then_inc(s["hid_done"], 1)

            x1_T(0)
            x1_T(1)
            hidden(0)
            for i in range(NQ + 2):
                if 1 <= i <= NQ:
                    k, p = i - 1, (i - 1) % 2
                    act.wait_ge(s["nmr2_done"], k + 1)
                    act.wait_ge(s["r2_done"], k + 1)
                    after(act, "y2T_done", k - 1)
                    after(act, "x2k_a", k - 1)
                    for g in range(GPQ):
                        last = act.activation(y2[:, p, g * D:(g + 1) * D], r2[:, p, g * D:(g + 1) * D], ACT.Identity,
                                              scale=ln2s[:, p, 1, g:g + 1], bias=ln2s[:, p, 3, g:g + 1])
                    last.then_inc(s["y2_done"], 1)
                if i + 1 < NQ:
                    hidden(i + 1)
                if i + 2 < NQ:
                    x1_T(i + 2)
                if 1 <= i <= NQ:
                    act.wait_ge(s["y2T_done"], k + 1)
                    after(act, "z_done3", k - 1)
                    after(act, "pool_done", k - 1)
                    act.activation(x2T[:, p, :], bk[4][:, :], ACT.Identity, scale=lnc[:, 0:1], bias=lnc[:, 1:2])\
                       .then_inc(s["x2T_done"], 1)
                if i >= 2:
                    gate_h1(i - 2)

        @block.vector
        def _(dve):
            dve.wait_ge(s["ld_ids"], 32)
            dve.tensor_copy(e1c[:, :], e1c_i[:, :])
            dve.tensor_copy(e1r[:, :], e1r_i[:, :]).then_inc(s["ids_f"], 1)
            dve.wait_ge(s["ld_const"], 16)
            dve.wait_ge(s["ids_f"], 1)
            dve.tensor_scalar(oh1r[:, :], e1r[:, :], const("part", E1), None, ALU.is_equal).then_inc(s["oh1r_done"], 1)
            dve.tensor_scalar(oh1[:, :], const("expert"), e1c[:, :], None, ALU.is_equal).then_inc(s["oh1_done"], 1)
            dve.wait_ge(s["oh1r_done"], 1)
            dve.reduce_sum(cnt[:, 0:1], oh1r[:, :], axis=AX.X).then_inc(s["cnt_done"], 1)
            dve.wait_ge(s["cnt_done"], 1)
            dve.tensor_scalar(cnt[:, 3:4], cnt[:, 0:1], 1.0 / Q, (Q - 1) / Q - (Q - 1) / (2 * Q), ALU.mult, ALU.add)\
               .then_inc(s["wcount_a"], 1)
            dve.wait_ge(s["wcount_a"], 1)
            dve.tensor_scalar(cnt[:, 1:2], cnt[:, 3:4], MAGIC, -MAGIC, ALU.add, ALU.add).then_inc(s["wcount_done"], 1)
            dve.wait_ge(s["ld_small"], 16 * 6)
            dve.tensor_scalar(ang[:, 2:4], ang[:, 0:2], 1.0 / (TWO_PI_HI + TWO_PI_LO), MAGIC, ALU.mult, ALU.add)\
               .then_inc(s["ang_a"], 1)
            dve.wait_ge(s["ang_a"], 1)
            dve.tensor_scalar(ang[:, 8:10], ang[:, 2:4], -MAGIC, None, ALU.add).then_inc(s["ang_b"], 1)
            dve.wait_ge(s["ang_b"], 1)
            dve.scalar_tensor_tensor(ang[:, 2:4], ang[:, 8:10], -TWO_PI_HI, ang[:, 0:2], ALU.mult, ALU.add)\
               .then_inc(s["ang_c"], 1)
            dve.wait_ge(s["ang_c"], 1)
            dve.scalar_tensor_tensor(ang[:, 4:6], ang[:, 8:10], -TWO_PI_LO, ang[:, 2:4], ALU.mult, ALU.add)\
               .then_inc(s["ang_d"], 1)
            dve.wait_ge(s["ang_d"], 1)
            dve.scalar_tensor_tensor(ang[:, 2:4], ang[:, 4:6], -1.0, ang[:, 4:6], ALU.mult, ALU.min).then_inc(s["ang_d"], 1)
            dve.wait_ge(s["ang_d"], 2)
            dve.tensor_scalar(ang[:, 6:8], ang[:, 2:4], float(3.14159265358979 / 2), None, ALU.add).then_inc(s["ang_e"], 1)

            dve.wait_ge(s["rank_mm"], 1)
            dve.tensor_tensor_reduce(out=rank[:, 0:E1], in0=bk[5][:, 0:E1], in1=oh1[:, :], scale=1.0, scalar=0.0,
                                     op0=ALU.mult, op1=ALU.add, accum_out=ang[:, 0:1]).then_inc(s["rank_done"], 1)
            dve.wait_ge(s["start_mm"], 1)
            dve.tensor_copy(cnt[:, 2:3], bk[4][0:E1, 500:501])
            dve.tensor_scalar(start4[:, :], bk[4][0:E1, 500:501], float(Q), None, ALU.mult).then_inc(s["start_done"], 1)
            dve.wait_ge(s["start_done"], 1)
            dve.tensor_tensor(cnt[:, 3:4], cnt[:, 2:3], cnt[:, 1:2], ALU.add).then_inc(s["end_done"], 1)
            dve.wait_ge(s["base_mm"], 1)
            dve.wait_ge(s["rank_done"], 1)
            dve.tensor_copy(ang[:, 1:2], bk[6][:, 0:1]).then_inc(s["base_done"], 1)
            dve.wait_ge(s["base_done"], 1)
            dve.tensor_scalar(place[:, :], const("slots"), ang[:, 0:1], ang[:, 1:2], ALU.subtract, ALU.is_equal)\
               .then_inc(s["place_done"], 1)
            dve.wait_ge(s["place_done"], 1)
            dve.scalar_tensor_tensor(placed[:, :], const("slots"), const("fromend"), place[:, :], ALU.add, ALU.mult)\
               .then_inc(s["placed_done"], 1)
            dve.tensor_scalar(ohw[:, 0, :], const("windows", E1), cnt[:, 2:3], None, ALU.is_ge)
            dve.wait_ge(s["end_done"], 1)
            dve.tensor_scalar(ohw[:, 1, :], const("windows", E1), cnt[:, 3:4], None, ALU.is_lt).then_inc(s["ohw_a"], 1)
            dve.wait_ge(s["ohw_a"], 1)
            dve.tensor_tensor(ohw[:, 0, :], ohw[:, 0, :], ohw[:, 1, :], ALU.mult).then_inc(s["ohw_done"], 1)
            dve.wait_ge(s["trig_done"], 1)
            dve.tensor_scalar(ang[:, 6:8], ang[:, 8:10], -1.0, None, ALU.mult).then_inc(s["nst_done"], 1)
            dve.wait_ge(s["nst_done"], 1)

            def perm_copy(k):
                dve.wait_ge(s["perm_mm"], k + 1)
                m = min(PS, S - k * PS)
                dve.tensor_copy(xT[:, :, k * PS:k * PS + m, :],
                                bk[k % 4][:, 0:m * NSLOT].rearrange("p (s w q) -> p w s q", s=m, q=Q)).then_inc(s["perm_dve"], 1)

            for k in range(NX):
                dve.wait_ge(s["rot_a"], k + 1)
                r = slice(k * SC, (k + 1) * SC)
                for o, i_, c in ((0, 1, 8), (1, 0, 6), (2, 3, 9), (3, 2, 7)):
                    last = dve.scalar_tensor_tensor(quad[:, r, :, o], quad_in[:, r, :, i_], ang[:, c:c + 1],
                                                    quad[:, r, :, o], ALU.mult, ALU.add)
                last.then_inc(s["rot_done"], 1)
                if k == 0:
                    dve.wait_ge(s["ew_mm"], 1)
                    dve.tensor_copy(ew_i[:, :], bk[5][0:1, 0:WP]).then_inc(s["ew_done"], 1)
                    dve.wait_ge(s["row_mm"], 1)
                    dve.tensor_tensor(row_i[:, :], bk[6][:, 0:W], const("rowbase"), ALU.add)\
                       .then_inc(s["row_done"], 1)
            for k in range(1, NPERM, 2):
                perm_copy(k)

            dve.tensor_copy(e2f[:, :], e2c_i[:, :])
            dve.tensor_copy(e2r[:, :], e2r_i[:, :]).then_inc(s["e2f_a"], 1)
            dve.wait_ge(s["e2f_a"], 1)
            dve.tensor_scalar(e2f[:, :], e2f[:, :], 1.0, 0.0, ALU.add, ALU.max)
            dve.tensor_scalar(e2r[:, :], e2r[:, :], 1.0, 0.0, ALU.add, ALU.max).then_inc(s["e2f_done"], 1)
            dve.wait_ge(s["e2f_done"], 1)
            dve.tensor_scalar(e2g_i[:, :], e2f[:, :], float(E2 - 1), None, ALU.min).then_inc(s["e2g_done"], 1)
            dve.tensor_scalar(oh2r[:, :], e2r[:, :], float(E2 - 1), const("part", E2), ALU.min, ALU.is_equal)\
               .then_inc(s["oh2r_done"], 1)
            dve.wait_ge(s["gram_mm"], 1)
            dve.tensor_copy(Z[:, 0:A], bk[7][0:2 * A, 0:A])
            dve.tensor_copy(Z[:, A:2 * A], const("eye32", 2 * A)).then_inc(s["z_done"], 1)
            dve.wait_ge(s["bias_mm"], 1)
            dve.tensor_copy(biasT[:, :], bk[7][:, 64:64 + B // Q]).then_inc(s["bias_done"], 1)
            dve.wait_ge(s["ew_done"], 1)
            dve_load, dve_expert = expert_regs(dve, "dve")
            dve.wait_ge(s["ld_vec"], 16)
            keep, rot = [0] * A, [(k + 1) % A for k in range(A)]

            def of_expert(w, k):
                return vec[:, bass.ds(dve_expert(w), 1), k, :].rearrange("p o d -> p (o d)")

            for w in range(SLOTS):
                j, v, u = w, w - 2, w - 3
                gs = j < A
                if gs:
                    dve.wait_ge(s["z_done"], j + 1)
                    dve.stream_shuffle(Zp[:, :], Z[:, :], keep).then_inc(s["piv_done"], 1)
                    dve.stream_shuffle(Zs[:, :], Z[:, :], rot).then_inc(s["zs_done"], 1)
                if 0 <= v < W:
                    dve_load(v)
                    dve.wait_ge(s["mm2_done"], v + 1)
                    after(dve, "yg_done", v - 1)
                    dve.tensor_tensor(r1[:, v % 2, :], OT[v % 2][:, 0:NP], of_expert(v, 0), ALU.add)\
                       .then_inc(s["r_done"], 1)
                if gs:
                    dve.wait_ge(s["zs_done"], j + 1)
                    a0 = c_at["lastrow"][0]
                    dve.tensor_tensor(gsv[:, 1:2], Zs[:, j:j + 1], cst[0:2 * A, a0 + j:a0 + j + 1], ALU.mult)\
                       .then_inc(s["t0_done"], 1)
                if 0 <= u < W:
                    dve.wait_ge(s["mv_done"], u + 1)
                    after(dve, "y1_done", u)
                    dve.scalar_tensor_tensor(yg[:, :], r1[:, u % 2, :], mv[:, u % 2, 0:1], of_expert(u, 1),
                                             ALU.subtract, ALU.mult).then_inc(s["yg_done"], 1)
                if 0 <= v < W:
                    dve.wait_ge(s["r_done"], v + 1)
                    dve.bn_stats(bst[:, :], r1[:, v % 2, :]).then_inc(s["bst_done"], 1)
                if gs:
                    dve.wait_ge(s["gpow_done"], j + 1)
                    dve.tensor_scalar(gsv[:, 2:3], gsv[:, 0:1], EPS3, None, ALU.add).then_inc(s["gadd_done"], 1)
                if 0 <= v < W:
                    dve.wait_ge(s["bst_done"], v + 1)
                    after(dve, "ve_done", v - 1)
                    dve.bn_aggr(mv[:, v % 2, :], bst[:, :]).then_inc(s["mv_done"], 1)
                if gs:
                    dve.wait_ge(s["gadd_done"], j + 1)
                    dve.reciprocal(gsv[:, 3:4], gsv[:, 2:3]).then_inc(s["grec_done"], 1)
                if 0 <= u < W:
                    dve.wait_ge(s["yg_done"], u + 1)
                    dve.wait_ge(s["rstd_done"], u + 1)
                    if u >= NY:
                        dve.wait_ge(s[f"y1_stored_{u % NY}"], 16 * (u // NY))
                    dve.scalar_tensor_tensor(y1[:, u % NY, :], yg[:, :], rstd[:, u % 2:u % 2 + 1], of_expert(u, 2),
                                             ALU.mult, ALU.add).then_inc(s["y1_done"], 1)
                if gs:
                    dve.wait_ge(s["grec_done"], j + 1)
                    dve.wait_ge(s["t0_done"], j + 1)
                    dve.tensor_scalar(gsv[:, 4:5], gsv[:, 1:2], gsv[:, 3:4], gsv[:, 3:4], ALU.mult, ALU.mult)\
                       .then_inc(s["t_done"], 1)
                    dve.wait_ge(s["t_done"], j + 1)
                    dve.scalar_tensor_tensor(Z[:, :], Zp[:, :], gsv[:, 4:5], Zs[:, :], ALU.mult, ALU.add)\
                       .then_inc(s["z_done"], 1)
                if w == POST - 1:
                    dve.wait_ge(s["z_done"], A + 1)
                    dve.tensor_tensor_reduce(out=Zp[:, 0:A], in0=Z[:, 0:A], in1=const("eye32", 2 * A), scale=1.0,
                                             scalar=0.0, op0=ALU.mult, op1=ALU.add, accum_out=gsv[:, 5:6])\
                       .then_inc(s["diag_done"], 1)
                if w == POST:
                    dve.wait_ge(s["dpow_done"], 1)
                    dve.tensor_scalar(gsv[:, 7:8], gsv[:, 6:7], EPS3, None, ALU.add).then_inc(s["dadd_done"], 1)
                    dve.wait_ge(s["dadd_done"], 1)
                    dve.reciprocal(gsv[:, 6:7], gsv[:, 7:8]).then_inc(s["drec_done"], 1)
                    dve.wait_ge(s["drec_done"], 1)
                    dve.tensor_scalar(Zs[:, 0:A], Z[:, A:2 * A], gsv[:, 6:7], None, ALU.mult).then_inc(s["ts_done"], 1)
                if w in (POST + 1, POST + 2):
                    k = w - POST - 1
                    full, rest = rrow[:, 2 + k, :], rrow[:, 3 if k == 0 else 0, :]
                    if k == 0:
                        dve.wait_ge(s["ld_l3"], 16 * N_L3)
                    else:
                        dve.wait_ge(s["rsp_done"], 1)
                        dve.tensor_tensor(full, rrow[:, 0, :], rrow[:, 1, :], ALU.add).then_inc(s["rrow_a"], 1)
                        dve.wait_ge(s["rrow_a"], 1)
                    dve.tensor_copy(rsp[:, k, 0, :], full).then_inc(s["rsp_a"], 1)
                    dve.wait_ge(s["rsp_a"], k + 1)
                    dve.tensor_tensor(rest, full, rsp[:, k, 0, :], ALU.subtract).then_inc(s["rsp_b"], 1)
                    dve.wait_ge(s["rsp_b"], k + 1)
                    dve.tensor_copy(rsp[:, k, 1, :], rest).then_inc(s["rsp_c"], 1)
                    dve.wait_ge(s["rsp_c"], k + 1)
                    dve.tensor_tensor(full, rest, rsp[:, k, 1, :], ALU.subtract).then_inc(s["rsp_d"], 1)
                    dve.wait_ge(s["rsp_d"], k + 1)
                    dve.tensor_copy(rsp[:, k, 2, :], full).then_inc(s["rsp_done"], 1)
            dve.tensor_scalar(hb2[:, :], gb2[:, :], 0.5, None, ALU.mult).then_inc(s["hb2_done"], 1)
            dve.wait_ge(s["saf_a"], 1)
            dve.tensor_scalar(saf[:, 0, :], saf[:, 1, :], 0.5 * KNOB, 0.5 * KNOB, ALU.mult, ALU.add).then_inc(s["saf_done"], 1)
            dve.wait_ge(s["saf_done"], 1)

            def pool_sum(k):
                p = k % 2
                dve.wait_ge(s["x2T_done"], k + 1)
                after(dve, "h1_mm", k - 1)
                dve.reduce_sum(pooled[:, p, :], x2T[:, p, :].rearrange("p (b s) -> p b s", s=S), axis=AX.X)\
                   .then_inc(s["pool_done"], 1)

            def finish(k):
                p = k % 2
                dve.wait_ge(s["tanh_done"], k + 1)
                dve.tensor_scalar(stg[:, 1, :], stg[:, 0, :], 0.5, 0.5, ALU.mult, ALU.add).then_inc(s["sig_done"], 1)
                dve.wait_ge(s["sig_done"], k + 1)
                dve.tensor_tensor(stt_[:, p, :], stg[:, 1, :], saf[:, 0, GPQ * k:GPQ * (k + 1)], ALU.mult)\
                   .then_inc(s["st_done"], 1)
                dve.wait_ge(s["st_done"], k + 1)
                dve.wait_ge(s["z_done3"], k + 1)
                dve.wait_ge(s["x2k_done"], k + 1)
                after(dve, "out_done", 16 * (k - 1))
                for g in range(GPQ):
                    last = dve.scalar_tensor_tensor(oS[:, p, g, :], bk[5][:, g * D:(g + 1) * D], stt_[:, p, g:g + 1],
                                                    x2k[:, p, g * D:(g + 1) * D], ALU.mult, ALU.add)
                last.then_inc(s["o_done"], 1)

            dve.wait_ge(s["eobd_zero"], 1)
            for i in range(NQ + 3):
                if i < NQ:
                    dve.wait_ge(s["eo_mm"], i + 1)
                    after(dve, "up_done", i)
                    for q in range(Q):
                        bb = biasT[A * q:A * q + A, GPQ * i:GPQ * (i + 1)].rearrange("p (g o) -> p g o", o=1)\
                            .broadcast_to([A, GPQ, S])
                        last = dve.tensor_tensor(eobd[A * q:A * q + A, :, q, :],
                                                 bk[1][A * q:A * q + A, 0:GPQ * S].rearrange("p (g s) -> p g s", g=GPQ),
                                                 bb, ALU.add)
                    last.then_inc(s["eobd_done"], 1)
                if i >= 3:
                    finish(i - 3)
                if i < NQ:
                    p = i % 2
                    dve.wait_ge(s["up_done"], i + 1)
                    dve.wait_ge(s[f"ld_x1_{i}"], 16)
                    after(dve, "y2_done", i - 1)
                    dve.tensor_tensor(r2[:, p, :], bk[2][:, :], x1k[:, i, :], ALU.add).then_inc(s["r2_done"], 1)
                    dve.wait_ge(s["r2_done"], i + 1)
                    for g in range(GPQ):
                        dve.bn_stats(bst2[:, g, :], r2[:, p, g * D:(g + 1) * D]).then_inc(s["bst2_done"], 1)
                    after(dve, "nmean2_done", i - 1)
                    for g in range(GPQ):
                        dve.wait_ge(s["bst2_done"], GPQ * i + g + 1)
                        last = dve.bn_aggr(mv2[:, p, g, :], bst2[:, g, :])
                    last.then_inc(s["mv2_done"], 1)
                    dve.wait_ge(s["mv2_done"], i + 1)
                if 1 <= i <= NQ:
                    pool_sum(i - 1)

        @block.tensor
        def _(pe):
            mm = pe.matmul
            pe.wait_ge(s["oh1_done"], 1)
            mm(bk[5][:, 0:E1], const("before"), oh1[:, :], start=True, stop=True).then_inc(s["rank_mm"], 1)
            pe.wait_ge(s["wcount_done"], 1)
            mm(bk[4][0:E1, 500:501], const("before8", E1), cnt[:, 1:2], start=True, stop=True).then_inc(s["start_mm"], 1)
            pe.wait_ge(s["start_done"], 1)
            mm(bk[6][:, 0:1], oh1r[:, :], start4[:, :], start=True, stop=True).then_inc(s["base_mm"], 1)
            pe.wait_ge(s["ld_small"], 16 * 6)
            for m in range(2):
                last = mm(bk[7][A * m:A * m + A, 0:A], uv_s[:, m, :], uv_s[:, m, :], start=True, stop=True)
            last.then_inc(s["gram_mm"], 1)
            pe.wait_ge(s["ohw_done"], 1)
            pe.wait_ge(s["rank_done"], 1)
            mm(bk[5][0:1, 0:WP], const("part", E1), ohw[:, 0, :], start=True, stop=True).then_inc(s["ew_mm"], 1)
            for c in range(IC):
                last = mm(bk[4][:, c * W:(c + 1) * W], bi_s[:, c * D:(c + 1) * D], ohw[:, 0, 0:W], start=True, stop=True)
            last.then_inc(s["bi_mm"], 1)
            pe.wait_ge(s["placed_done"], 1)
            a0 = c_at["rowmat"][0]
            for q in range(Q):
                last = mm(bk[6][:, 0:W], cst[:, a0 + q * NP:a0 + (q + 1) * NP],
                          placed[:, :].rearrange("b (w q) -> b w q", q=Q)[:, :, q], start=(q == 0), stop=(q == Q - 1))
            last.then_inc(s["row_mm"], 1)
            for k in range(NPERM):
                for t in range(k * PS, min(S, (k + 1) * PS)):
                    if t % SC == 0:
                        pe.wait_ge(s["rot_done"], t // SC + 1)
                    if t == k * PS and k >= 4:
                        pe.wait_ge(s["perm_act" if k % 2 == 0 else "perm_dve"], k // 2 - 1)
                    last = mm(bk[k % 4][:, (t - k * PS) * NSLOT:(t - k * PS + 1) * NSLOT], xr[:, t, :], place[:, :],
                              start=True, stop=True)
                last.then_inc(s["perm_mm"], 1)
            pe.wait_ge(s["oh2r_done"], 1)
            pe.wait_ge(s["ld_l2"], 16 * 5)
            pe.wait_ge(s["z_done"], 1)
            for q in range(Q):
                mm(bk[7][A * q:A * q + A, 64:64 + B // Q], dbt[:, :], oh2r[:, q:B:Q], start=True, stop=False)
                last = mm(bk[7][A * q:A * q + A, 64:64 + B // Q], det[:, :], oh2r[:, q:B:Q], start=False, stop=True)
            last.then_inc(s["bias_mm"], 1)
            pe.wait_ge(s["perm_act"], (NPERM + 1) // 2)
            pe.wait_ge(s["perm_dve"], NPERM // 2)
            pe.wait_ge(s["bi_done"], 1)
            pe.wait_ge(s["ew_done"], 1)
            pe.wait_ge(s["bias_done"], 1)
            pe_load, pe_expert = expert_regs(pe, "pe")

            def up_to_tokens(w):
                pe_load(w)
                e = pe_expert(w)
                after(pe, "r_done", w - 1)
                mm(OT[w % 2][:, 0:NP], xT[:, w, :, :].rearrange("p s q -> p (s q)"), ident, start=True, stop=False)
                for c in range(IC):
                    pe.wait_ge(s["gelu_done"], w * IC + c + 1)
                    last = mm(OT[w % 2][:, 0:NP], hT[:, w % 2, c * NP:(c + 1) * NP],
                              bank[:, bass.ds(e, 1), 1, c * D:(c + 1) * D].rearrange("p o d -> p (o d)"),
                              start=False, stop=(c == IC - 1))
                last.then_inc(s["mm2_done"], 1)

            def post(n):
                t7 = bk[7]
                if n == 1:
                    pe.wait_ge(s["ts_done"], 1)
                    last = pe.transpose(t7[0:A, 0:2 * A], Zs[:, 0:A], cst[0:2 * A, 0:2 * A])
                elif n == 2:
                    pe.wait_ge(s["post_cp"], 1)
                    mm(t7[0:A, 0:D], tt_s[:, 0, :], uvt_s[:, 0, :], start=True, stop=True)
                    mm(t7[0:A, D:D + A], uvt_s[:, 0, 0:A], tt_s[:, 0, :], start=True, stop=True)
                    last = mm(t7[:, D + A:D + 2 * A], uvt_s[:, 1, :], tt_s[:, 1, :], start=True, stop=True)
                elif n == 3:
                    pe.wait_ge(s["post_cp"], 2)
                    pe.wait_ge(s["ld_l3"], 16 * N_L3)
                    mm(t7[0:A, 0:A], vo[:, :], vo[:, :], start=True, stop=True)
                    last = mm(t7[0:A, A:A + D], ur[:, :], rwt[:, :], start=True, stop=True)
                elif n == 4:
                    pe.wait_ge(s["post_cp"], 3)
                    last = mm(t7[0:A, 0:D], vv[:, :], p1[:, :], start=True, stop=True)
                else:
                    pe.wait_ge(s["post_cp"], 4)
                    last = mm(t7[:, 0:D], uo_t[:, :], fm[:, :], start=True, stop=True)
                last.then_inc(s["post_pe"], 1)

            for w in range(SLOTS):
                if w < W:
                    pe.wait_ge(s["wi_staged"], w + 1)
                    for c in range(IC):
                        if c % 2 == 0:
                            after(pe, "gelu_done", (w - 2) * IC + c + 2)
                        last = mm(H[w % 2][c // 2][:, (c % 2) * NP:(c % 2 + 1) * NP], wi_st[:, w % 2, c * D:(c + 1) * D],
                                  xT[:, w, :, :].rearrange("p s q -> p (s q)"), start=True, stop=True)
                        if c % 2 == 1:
                            last.then_inc(s["mm1_done"], 1)
                if w == 1:
                    pe.wait_ge(s["ld_wo"], 16 * E1)
                if 0 <= w - 1 < W:
                    up_to_tokens(w - 1)
                if POST < w <= POST + 5:
                    post(w - POST)
            def load_T(i):
                pe.wait_ge(s[f"ld_x1_{i}"], 16)
                after(pe, "x1T_done", i)
                for g in range(GPQ):
                    last = pe.transpose(bk[6][:, g * D:(g + 1) * D], x1k[:, i, g * D:(g + 1) * D], ident)
                last.then_inc(s["xp_done"], 1)

            def down(i):
                pe.wait_ge(s["x1T_done"], i + 1)
                after(pe, "hid_done", i)
                v = x1T[:, i % 2, :].rearrange("p (g q s) -> p g q s", g=GPQ, q=Q)
                for q in range(Q):
                    last = mm(bk[0][A * q:A * q + A, 0:GPQ * S], dwt[:, :], v[:, :, q, :], start=True, stop=True)
                last.then_inc(s["down_done"], 1)

            def expert(i):
                pe.wait_ge(s["hid_done"], i + 1)
                after(pe, "eobd_done", i)
                for g in range(GPQ):
                    last = mm(bk[1][:, g * S:(g + 1) * S], dW[:, GPQ * i + g, :, :].rearrange("p q o -> p (q o)"),
                              hid[:, i % 2, g * S:(g + 1) * S], start=True, stop=True)
                last.then_inc(s["eo_mm"], 1)

            def bias(bank_, k):
                mm(bank_[:, :], ones3[:, :], rb3[:, k, :].rearrange("k (o d) -> k o d", o=1).broadcast_to([3, GPQ, D]),
                   start=True, stop=False)

            def up(i):
                after(pe, "r2_done", i)
                bias(bk[2], 0)
                pe.wait_ge(s["eobd_done"], i + 1)
                for g in range(GPQ):
                    last = mm(bk[2][:, g * D:(g + 1) * D], eobd[:, g, :, :].rearrange("p q s -> p (q s)"), ut4[:, :],
                              start=False, stop=(g == GPQ - 1))
                last.then_inc(s["up_done"], 1)

            def back(i):
                pe.wait_ge(s["y2_done"], i + 1)
                after(pe, "x2T_done", i)
                for g in range(GPQ):
                    last = pe.transpose(bk[4][:, g * D:(g + 1) * D], y2[:, i % 2, g * D:(g + 1) * D], ident)
                last.then_inc(s["y2T_done"], 1)

            def response(i):
                pe.wait_ge(s["pool_done"], i + 1)
                after(pe, "tanh_done", i)
                mm(bk[7][0:R, 0:GPQ * Q], gw1[:, :], pooled[:, i % 2, :], start=True, stop=True).then_inc(s["h1_mm"], 1)
                after(pe, "o_done", i)
                bias(bk[5], 1)
                for g in range(GPQ):
                    last = mm(bk[5][:, g * D:(g + 1) * D], x2T[:, i % 2, g * D:(g + 1) * D], M[:, :], start=False,
                              stop=(g == GPQ - 1))
                last.then_inc(s["z_done3"], 1)

            def strength(i):
                pe.wait_ge(s["h1_done"], i + 1)
                for q in range(Q):
                    last = mm(bk[7][S * q:S * q + S, 64:64 + GPQ], gw2[:, 0:1].broadcast_to([R, S]),
                              h1[:, i % 2, q:GPQ * Q:Q], start=True, stop=True)
                last.then_inc(s["st_mm"], 1)

            pe.wait_ge(s["rb3_done"], 16 * 6)
            pe.wait_ge(s["dW_done"], 16 * Q)
            pe.wait_ge(s["half_done"], 1)
            pe.wait_ge(s["post_cp"], 5)
            load_T(0)
            load_T(1)
            down(0)
            for i in range(NQ + 2):
                if i < NQ:
                    expert(i)
                if i + 1 < NQ:
                    down(i + 1)
                if i + 2 < NQ:
                    load_T(i + 2)
                if 1 <= i <= NQ:
                    back(i - 1)
                if i < NQ:
                    up(i)
                if i >= 2:
                    response(i - 2)
                    strength(i - 2)


N_L3 = 10


def kernel(**inputs):
    import numpy as np
    import concourse.bacc as bacc
    from concourse import mybir
    from concourse.bass_utils import run_bass_kernel_spmd

    a = {k: np.asarray(v) for k, v in inputs.items()}
    f = np.float32
    B, S, D = a["x"].shape
    E1, E2 = a["L1_cond_Wi"].shape[0], a["L2_cond_expert_W"].shape[0]
    A = a["L2_cond_down_W"].shape[0]
    Q = 4
    W = (B + E1 * (Q - 1)) // Q
    NSLOT = W * Q
    p = np.arange(128)
    lastrow = np.where((p[:, None] % A) <= A - 2 - np.arange(A)[None], -1.0, 0.0)
    WP = -(-W // 4) * 4
    rowmat = np.concatenate([-S * np.ones((128, 1)) * (p[None, :] % Q == q) for q in range(Q)], axis=1)
    rowbase = S * (B + Q * np.arange(W)[None] + p[:, None] % Q) + p[:, None] // Q
    const = np.concatenate([
        np.eye(128), (p[:, None] < p[None, :]), np.tile(np.arange(NSLOT), (128, 1)), np.tile(np.arange(E1), (128, 1)),
        p[:, None], lastrow, np.eye(A)[p % A], (p[:, None] < np.arange(E1)[None]),
        np.tile(np.arange(WP), (128, 1)), rowmat, rowbase, B - p[:, None]], axis=1).astype(f)
    eye = np.eye(A, dtype=f).reshape(1, A * A)
    wt = a["L2_cond_expert_W"].transpose(0, 2, 1).reshape(E2, A * A)
    zero = np.zeros((1, A), f)
    emb = a["L2_cond_domain_emb"]
    l1_vec = np.stack([a["L1_cond_bo"], a["L1_cond_gamma"], a["L1_cond_beta"]], axis=1)
    ins = {
        "x": a["x"],
        "expert1_col": a["itok_B_0_7"].reshape(B, 1), "expert1_row": a["itok_B_0_7"],
        "expert2_col": a["itok_B_0_15"].reshape(B, 1), "expert2_row": a["itok_B_0_15"],
        "angles": np.stack([a["condB_theta"], a["condB_phi"]], axis=1),
        "safety_tok": np.repeat(a["condB_safetyscore"].reshape(B // Q, Q).T, S, axis=0),
        "l1_wi": a["L1_cond_Wi"], "l1_wo": a["L1_cond_Wo"], "l1_bi": a["L1_cond_bi"], "l1_vec": l1_vec,
        "down_wt": a["L2_cond_down_W"].T, "down_b4": np.tile(a["L2_cond_down_b"], Q).reshape(Q * A, 1),
        "up_t4": np.tile(a["L2_cond_up_W"].T, (Q, 1)), "up_b": a["L2_cond_up_b"].reshape(1, 1, D),
        "dom_w": np.concatenate([eye, wt, eye]),
        "dom_b": np.concatenate([zero, a["L2_cond_expert_b"], zero]),
        "dom_e": np.concatenate([emb[:1], emb, emb[-1:]]),
        "ln_cols": np.stack([a["L2_cond_ln_gamma"], a["L2_cond_ln_beta"]], axis=1),
        "ln_rows": np.stack([a["L2_cond_ln_gamma"], a["L2_cond_ln_beta"]]),
        "uv": np.stack([a["L3_cond_U"], a["L3_cond_V"]], axis=1),
        "uv_t": np.stack([a["L3_cond_U"].T, a["L3_cond_V"].T], axis=1),
        "gate_w1t": a["L3_cond_gate_w1"].T, "gate_b1": a["L3_cond_gate_b1"].reshape(-1, 1),
        "gate_w2": a["L3_cond_gate_w2"].reshape(-1, 1), "gate_b2": a["L3_cond_gate_b2"],
        "resp_wt": a["L3_cond_resp_w"].T,
        "resp_rows": np.stack([a["L3_cond_resp_b"], a["L3_cond_safety_bias"]]).reshape(1, 2, D),
        "const_f": const,
    }
    nc = bacc.Bacc("TRN2", target_bir_lowering=False, num_devices=1)
    arrays, args = {}, {}
    for name, v in ins.items():
        v = np.ascontiguousarray(v)
        arrays[f"in_{name}"] = v
        args[name] = nc.dram_tensor(f"in_{name}", v.shape, mybir.dt.from_np(v.dtype), kind="ExternalInput").ap()
    out = nc.dram_tensor("out_0", (B, S, D), mybir.dt.float32, kind="ExternalOutput").ap()
    cond_seq_program(nc, out=out, **args)
    r = run_bass_kernel_spmd(nc, [arrays], core_ids=[0])
    return r.results[0]["out_0"]
```

```python
import concourse.bass as bass
from concourse import mybir
from contextlib import ExitStack


def cond_seq_program(nc, x, expert1_col, expert1_row, expert2_col, expert2_row, angles, l1_w, l1_vec,
                     dom_w, rows, ln_rows, const_f, tokmask, params, param_at, out):
    f32, bf16, i32 = mybir.dt.float32, mybir.dt.bfloat16, mybir.dt.int32
    ALU, ACT, AX = mybir.AluOpType, mybir.ActivationFunctionType, mybir.AxisListType

    B, S, D = x.shape
    E1 = l1_w.shape[2]
    E3 = 3 * E1
    IC = l1_w.shape[3] // D
    A = param_at["down_wt"][2]
    E2 = dom_w.shape[0]
    R = param_at["gate_w1t"][2]
    Q = 4
    W = (B + E1 * (Q - 1)) // Q
    NSLOT = W * Q
    WP = -(-W // 4) * 4
    NP = 128
    SC = 8
    NX = S // SC
    PS = 3
    NPERM = (S + PS - 1) // PS
    NK = 4
    NY = 4
    GPQ = 4
    NQ = B * S // (NP * GPQ)
    TQ = NP * GPQ
    TWO_PI_HI, TWO_PI_LO = 6.28125, 0.0019353071795864769
    MAGIC = float(3 * 2 ** 22)
    EPS1, EPS2, EPS3 = 1e-12, 1e-5, 1e-8
    KNOB = min(max(1.0, 0.1), 1.0)

    c_at, c_n = {}, 0
    for name, n in (("ident", NP), ("before", B), ("slots", NSLOT), ("expert", E1), ("part", 1), ("lastrow", A),
                    ("eye32", A), ("before8", E3), ("part3", 1), ("third", 3), ("in_group", GPQ), ("windows", WP), ("fromend", 1), ("rowbase", W), ("ones", 1)):
        c_at[name] = (c_n, c_n + n)
        c_n += n

    ctx = ExitStack()
    with ctx:
        def sb(name, shape, dt=f32):
            return ctx.enter_context(nc.sbuf_tensor(name, shape, dt))

        def sem(name):
            return ctx.enter_context(nc.semaphore(name))

        cst = sb("cst", [NP, c_n])

        def const(name, p=NP):
            a, b = c_at[name]
            return cst[0:p, a:b]

        ident = const("ident")
        mask = sb("mask", [1, Q * NP])
        pl_row = sb("pl_row", [1, NSLOT])
        prm = sb("prm", [NP, params.shape[1]])

        def param(name):
            p, a, n = param_at[name]
            return prm[0:p, a:a + n]

        safety, uv_s, uvt_s, bi_s = param("safety"), param("uv"), param("uv_t"), param("l1_bi")
        dwt, db4, ut4 = param("down_wt"), param("down_b4"), param("up_t4")
        dbt, det, lnc = param("dom_b"), param("dom_e"), param("ln_cols")
        gw1, gb1, gw2, gb2, rwt = (param(n) for n in ("gate_w1t", "gate_b1", "gate_w2", "gate_b2", "resp_wt"))
        xb = sb("xb", [B, S, D])
        xr = sb("xr", [B, S, D])
        xT = sb("xT", [D, W, S, Q])
        bank = sb("bank", [D, 2, E1, IC * D])
        vec = sb("vec", [NP, E1, 2, D])
        oh16 = sb("oh16", [E3, WP], bf16)
        bo_rest, bo3 = sb("bo_rest", [E3, 2, D]), sb("bo3", [E3, 3, D], bf16)
        bo24 = sb("bo24", [E3, 3, D], bf16)
        wi_st = sb("wi_st", [D, 2, IC * D])
        e1c_i, e2c_i = sb("e1c_i", [B, 1], i32), sb("e2c_i", [B, 1], i32)
        e1r_i, e2r_i = sb("e1r_i", [E3, B], i32), sb("e2r_i", [E2, B], i32)
        e1c, e1r, e2r = sb("e1c", [B, 1]), sb("e1r", [E3, B]), sb("e2r", [E2, B])
        e2f, e2g_i = sb("e2f", [B, 1]), sb("e2g_i", [B, 1], i32)
        oh1 = sb("oh1", [B, E1])
        oh1r = sb("oh1r", [E3, B])
        oh2r = sb("oh2r", [E2, B])
        cnt = sb("cnt", [E3, 4])
        start4 = sb("start4", [E3, 1])
        ohw = sb("ohw", [E3, 2, WP])
        rank = sb("rank", [B, 8])
        placed = sb("placed", [B, NSLOT])
        place = sb("place", [B, NSLOT])
        row_i = sb("row_i", [NP, W], i32)
        ew_i = sb("ew_i", [1, WP], i32)
        ang = sb("ang", [B, 12])
        biW = sb("biW", [D, IC, W])
        hT = sb("hT", [D, 2, IC * NP])
        bst, mv = sb("bst", [NP, 6]), sb("mv", [NP, 2, 2])
        ve, rstd = sb("ve", [NP, 2]), sb("rstd", [NP, 2])
        yg = sb("yg", [NP, D])
        y1 = sb("y1", [NP, NY, D])
        mhalf = sb("mhalf", [NP, GPQ])
        phalf = sb("phalf", [NP, 1])
        Z, Zp, Zs = sb("Z", [2 * A, 2 * A]), sb("Zp", [2 * A, 2 * A]), sb("Zs", [2 * A, 2 * A])
        gsv = sb("gsv", [2 * A, 8])
        dG = sb("dG", [B, A * A])
        dW = sb("dW", [NP, B // Q, Q, A])
        brow, brest = sb("brow", [B // Q, NP]), sb("brest", [B // Q, 2, NP])
        bparts = sb("bparts", [B // Q, 3, NP], bf16)
        brow3 = sb("brow3", [3 * GPQ, NQ, NP], bf16)
        in_group = sb("in_group", [3 * GPQ, GPQ, S], bf16)
        x1k = xb[:, :, :].rearrange("p s d -> p (s d)").rearrange("p (i n) -> p i n", i=NQ)
        x1T = sb("x1T", [D, 2, TQ])
        hid = sb("hid", [NP, 2, GPQ * S])
        eobd = sb("eobd", [NP, GPQ, Q, S])
        r2 = sb("r2", [NP, 2, TQ])
        bst2, mv2 = sb("bst2", [NP, GPQ, 6]), sb("mv2", [NP, 2, GPQ, 2])
        ln2s = sb("ln2s", [NP, 2, 4, GPQ])
        y2 = sb("y2", [NP, 2, TQ])
        lnr = sb("lnr", [NP, 2, D])
        x2T = sb("x2T", [D, 2, TQ])
        x2k = sb("x2k", [NP, NK, TQ])
        tt_s = sb("tt_s", [A, 2, A])
        uo_t, ur, vo = sb("uo_t", [A, D]), sb("ur", [A, A]), sb("vo", [D, A])
        vv, p1, fm = sb("vv", [A, A]), sb("p1", [A, D]), sb("fm", [A, D])
        M = sb("M", [D, D])
        rrow = sb("rrow", [1, 8, D])
        rsp = sb("rsp", [1, 2, 3, D], bf16)
        rb3, ones3 = sb("rb3", [3, 2, D], bf16), sb("ones3", [3, NP], bf16)
        hb2 = sb("hb2", [NP, 1])
        zeros = sb("zeros", [NP, 512])
        junk = sb("junk", [NP, 1])
        saf = sb("saf", [NP, 2, B // Q])
        pooled = sb("pooled", [D, 2, GPQ * Q])
        h1 = sb("h1", [R, 2, GPQ * Q])
        stg = sb("stg", [NP, 1, GPQ])
        stt_ = sb("stt_", [NP, 2, GPQ])
        oS = sb("oS", [NP, 2, GPQ, D])

        bk = [ctx.enter_context(nc.psum_tensor(f"bank{i}", [128, 512], f32)) for i in range(8)]

        names = """ld_const ld_ids ld_ang ld_mask ld_prm ld_wi ld_wo ld_vec ld_rows ld_ids2 ids_f oh1_done oh1r_done oh2r_done
            cnt_done wcount_a wcount_done start_mm start_done end_done ohw_a ohw_done rank_mm rank_done
            base_mm base_done place_done placed_done pl_mm pl_done ew_mm ew_done row_mm row_done bi_mm bi_done
            ang_a ang_b ang_c ang_d ang_e trig_done nst_done rot_a rot_done perm_mm perm_act perm_dve
            wi_staged mm1_done gelu_done mm2_done oh16_done bo24_done bst_done mv_done ve_done rstd_done yg_done y1_done
            half_done junk_done gram_mm z_done piv_done zs_done gpow_done t0_done gadd_done grec_done t_done
            diag_done dpow_done dadd_done drec_done ts_done post_pe post_cp e2f_a e2f_done e2g_done
            dG_done dwd_done dW_zero dW_done bias_mm bias_done bpd_done brow3_done in_group_done eobd_done eobd_zero zeros_done xp_done x1T_done down_done hid_done
            eo_mm up_done r2_done bst2_done mv2_done ve2_done rstd2_done nmean2_done
            nmr2_done y2_done y2T_done x2T_done pool_done x2k_a x2k_done z_done3 h1_mm h1_done st_mm
            tanh_done st_done o_done out_done rrow_a rsp_a rsp_b rsp_c rsp_d rsp_done
            rb3_done hb2_done saf_a saf_done""".split()
        s = {n: sem(n) for n in names + [f"ld_x{k}" for k in range(NX)]
             + [f"ld_x1_{k}" for k in range(NQ)] + [f"y1_stored_{k}" for k in range(NY)]}

        def after(eng, name, n):
            if not isinstance(n, int) or n > 0:
                eng.wait_ge(s[name], n)

        def ld(eng, dst, src, name):
            eng.dma_start(dst, src).then_inc(s[name], 16)

        x1_dram = nc.dram_tensor("layer1_out", ((B + NSLOT) * S, D), f32, kind="Internal").ap()
        dw_dram = nc.dram_tensor("dw_by_batch", (B, A * A), f32, kind="Internal").ap()
        bp_dram = nc.dram_tensor("domain_bias_parts", (B // Q, 3, NP), bf16, kind="Internal").ap()
        block = ctx.enter_context(nc.Block())
        H = [[bk[0], bk[1]], [bk[2], bk[3]]]
        OT = [bk[4], bk[5], bk[6]]
        Z3 = [bk[3], bk[5]]

        def blocks(q):
            return bk[1][A * q:A * q + A, 0:GPQ * S].rearrange("p (g s) -> p g s", g=GPQ)

        def expert_regs(eng, name):
            regs = [[eng.alloc_register(f"{name}{k}{j}") for j in range(4)] for k in range(2)]

            def load(w):
                if w % 4 == 0:
                    eng.load(regs[w // 4 % 2], ew_i[0:1, w:w + 4])

            def at(w):
                return eng.snap(regs[w // 4 % 2][w % 4], min_val=0, max_val=E1 - 1)
            return load, at

        SLOTS = W + 4
        POST = A + 1

        def all_y1_stored(eng):
            for k in range(NY):
                eng.wait_ge(s[f"y1_stored_{k}"], 16 * len(range(k, W, NY)))

        def load_x1(eng, quads):
            for i in quads:
                ld(eng, x1k[:, i, :].rearrange("p (g d) -> p g d", g=GPQ),
                   x1_dram[TQ * i:TQ * (i + 1)].rearrange("(g p) d -> p g d", p=NP), f"ld_x1_{i}")

        @block.sync
        def _(sp):
            ld(sp, e1c_i[:, :], expert1_col, "ld_ids")
            ld(sp, ang[:, 0:2], angles, "ld_ang")
            for k in range(NX):
                ld(sp, xb[:, k * SC:(k + 1) * SC, :], x[:, k * SC:(k + 1) * SC, :], f"ld_x{k}")
            ld(sp, prm[:, :], params, "ld_prm")
            ld(sp, bank[:, 0, :, :], l1_w[:, 0], "ld_wi")
            ld(sp, bank[:, 1, :, :], l1_w[:, 1], "ld_wo")
            ld(sp, vec[:, :, :, :], l1_vec.partition_broadcast(NP), "ld_vec")
            ld(sp, e2c_i[:, :], expert2_col, "ld_ids2")
            ld(sp, e2r_i[:, :], expert2_row.partition_broadcast(E2), "ld_ids2")
            sp.wait_ge(s["dG_done"], 16)
            ld(sp, dw_dram, dG[:, :], "dwd_done")
            sp.wait_ge(s["dwd_done"], 16)
            sp.wait_ge(s["dW_zero"], 1)
            for q in range(Q):
                ld(sp, dW[A * q:A * q + A, :, q, :],
                   dw_dram.rearrange("(g q) (a o) -> q a g o", q=Q, a=A)[q], "dW_done")
            sp.wait_ge(s["rsp_done"], 2)
            ld(sp, bp_dram, bparts[:, :, :], "bpd_done")
            sp.wait_ge(s["bpd_done"], 16)
            ld(sp, brow3[:, :, :], bp_dram.rearrange("(i g) k n -> (g k) i n", g=GPQ), "brow3_done")
            all_y1_stored(sp)
            load_x1(sp, range(1, 3))
            sp.wait_ge(s["rsp_done"], 4)
            for k in range(2):
                for j in range(3):
                    ld(sp, rb3[j:j + 1, k, :], rsp[0:1, k, j, :], "rb3_done")
            load_x1(sp, range(3, NQ))
            for i in range(NQ):
                sp.wait_ge(s["o_done"], i + 1)
                after(sp, "out_done", 16 * i)
                sp.dma_start(out[Q * GPQ * i:Q * GPQ * (i + 1)].rearrange("(g q) s d -> (q s) g d", q=Q),
                             oS[:, i % 2, :, :]).then_inc(s["out_done"], 16)
            sp.wait_ge(s["out_done"], 16 * NQ)

        @block.gpsimd
        def _(pool):
            pool.memset(zeros[:, :], 0.0).then_inc(s["zeros_done"], 1)
            pool.memset(mhalf[:, :], -0.5)
            pool.memset(phalf[:, :], 0.5)
            pool.memset(ones3[:, :], 1.0).then_inc(s["half_done"], 1)
            pool.memset(eobd[:, :, :, :], 0.0).then_inc(s["eobd_zero"], 1)
            pool.memset(dW[:, :, :, :], 0.0).then_inc(s["dW_zero"], 1)
            pool.wait_ge(s["half_done"], 1)
            pool.wait_ge(s["row_done"], 1)
            for w in range(SLOTS + 1):
                if w < A:
                    pool.wait_ge(s["piv_done"], w + 1)
                    pool.tensor_tensor(gsv[:, 0:1], Zp[:, w:w + 1], phalf[0:2 * A, :], ALU.pow)\
                        .then_inc(s["gpow_done"], 1)
                v = w - 4
                if 0 <= v < W:
                    pool.wait_ge(s["y1_done"], v + 1)
                    pool.indirect_dma_start(x1_dram, bass.IndirectOffsetOnAxis(row_i[:, v:v + 1], 0),
                                            y1[:, v % NY, :], None).then_inc(s[f"y1_stored_{v % NY}"], 16)
                v = w - 2
                if 0 <= v < W:
                    p = v % 2
                    pool.wait_ge(s["ve_done"], v + 1)
                    if v >= NY:
                        pool.wait_ge(s[f"y1_stored_{v % NY}"], 16 * (v // NY))
                    pool.tensor_tensor(rstd[:, p:p + 1], ve[:, p:p + 1], mhalf[:, 0:1], ALU.pow)\
                        .then_inc(s["rstd_done"], 1)
                if w == 2:
                    pool.wait_ge(s["e2g_done"], 1)
                    pool.indirect_dma_start(dG[:, :], None, dom_w,
                                            bass.IndirectOffsetOnAxis(e2g_i[:, 0:1], 0)).then_inc(s["dG_done"], 16)

                if w == POST - 1:
                    pool.wait_ge(s["diag_done"], 1)
                    pool.tensor_tensor(gsv[:, 6:7], gsv[:, 5:6], phalf[0:2 * A, :], ALU.pow).then_inc(s["dpow_done"], 1)

            g2 = lnr[:, 0, :].rearrange("p (o d) -> p o d", o=1).broadcast_to([NP, GPQ, D])
            b2 = lnr[:, 1, :].rearrange("p (o d) -> p o d", o=1).broadcast_to([NP, GPQ, D])
            pool.wait_ge(s["ld_rows"], 16 * 2)
            def rstd2(i):
                p = i % 2
                after(pool, "y2_done", i - 1)
                pool.wait_ge(s["ve2_done"], i + 1)
                pool.tensor_tensor(ln2s[:, p, 1, :], ln2s[:, p, 0, :], mhalf[:, :], ALU.pow).then_inc(s["rstd2_done"], 1)
                pool.wait_ge(s["nmean2_done"], i + 1)
                pool.wait_ge(s["rstd2_done"], i + 1)
                pool.tensor_tensor(ln2s[:, p, 3, :], ln2s[:, p, 2, :], ln2s[:, p, 1, :], ALU.mult).then_inc(s["nmr2_done"], 1)

            def scale_shift(k):
                p = k % 2
                pool.wait_ge(s["y2_done"], k + 1)
                after(pool, "o_done", k - NK + 1)
                v = x2k[:, k % NK, :].rearrange("p (g d) -> p g d", g=GPQ)
                pool.tensor_tensor(v, y2[:, p, :].rearrange("p (g d) -> p g d", g=GPQ), g2, ALU.mult).then_inc(s["x2k_a"], 1)
                pool.wait_ge(s["x2k_a"], k + 1)
                pool.tensor_tensor(v, v, b2, ALU.add).then_inc(s["x2k_done"], 1)

            for t in range(NQ + 1):
                if 0 <= t < NQ:
                    rstd2(t)
                if 0 <= t - 1 < NQ:
                    scale_shift(t - 1)

        quad = xr[:, :, :].rearrange("b s (k r) -> b s k r", r=4)
        quad_in = xb[:, :, :].rearrange("b s (k r) -> b s k r", r=4)

        @block.scalar
        def _(act):
            ld(act, e1r_i[:, :], expert1_row.partition_broadcast(E3), "ld_ids")
            ld(act, cst[:, :], const_f, "ld_const")
            ld(act, mask[:, :], tokmask, "ld_mask")
            act.wait_ge(s["half_done"], 1)
            act.activation(junk[:, :], mhalf[:, 0:1], ACT.Sin).then_inc(s["junk_done"], 1)
            act.wait_ge(s["ang_e"], 1)
            act.activation(ang[:, 8:12], ang[:, 4:8], ACT.Sin).then_inc(s["trig_done"], 1)
            act.wait_ge(s["trig_done"], 1)
            for k in range(NX):
                act.wait_ge(s[f"ld_x{k}"], 16)
                r = slice(k * SC, (k + 1) * SC)
                act.activation(quad[:, r, :, 0:2], quad_in[:, r, :, 0:2], ACT.Copy, scale=ang[:, 10:11])
                act.activation(quad[:, r, :, 2:4], quad_in[:, r, :, 2:4], ACT.Copy, scale=ang[:, 11:12])\
                   .then_inc(s["rot_a"], 1)
            for dst, src in ((lnr[:, :, :], ln_rows.partition_broadcast(NP)), (rrow[:, 0:3, :], rows)):
                ld(act, dst, src, "ld_rows")
            act.wait_ge(s["junk_done"], 1)
            act.activation(junk[:, :], mhalf[:, 0:1], ACT.Gelu).then_inc(s["junk_done"], 1)
            act_load, act_expert = expert_regs(act, "act")

            def stage(w):
                act_load(w)
                e = act_expert(w)
                after(act, "mm1_done", 2 * (w - 1))
                act.activation(wi_st[:, w % 2, :], bank[:, 0, bass.ds(e, 1), :].rearrange("p o n -> p (o n)"), ACT.Copy)\
                   .then_inc(s["wi_staged"], 1)

            for k in range(0, NPERM, 2):
                if k == 8:
                    act.wait_ge(s["bi_mm"], 1)
                    act.activation(biW[:, :, :].rearrange("p c w -> p (c w)"), bk[4][:, 0:IC * W], ACT.Copy)\
                       .then_inc(s["bi_done"], 1)
                if k == 10:
                    act.wait_ge(s["ew_done"], 1)
                    act.wait_ge(s["ld_wi"], 16)
                    stage(0)
                act.wait_ge(s["perm_mm"], k + 1)
                m = min(PS, S - k * PS)
                act.activation(xT[:, :, k * PS:k * PS + m, :],
                               bk[k % 4][:, 0:m * NSLOT].rearrange("p (s w q) -> p w s q", s=m, q=Q), ACT.Copy).then_inc(s["perm_act"], 1)
            def copies(n):
                act.wait_ge(s["post_pe"], n)
                for dst, src in (((tt_s[:, :, :].rearrange("k m r -> k (m r)"), bk[7][0:A, 0:2 * A]),),
                                 ((uo_t[:, :], bk[7][0:A, 0:D]), (ur[:, :], bk[7][0:A, D:D + A]),
                                  (vo[:, :], bk[7][:, D + A:D + 2 * A])),
                                 ((vv[:, :], bk[7][0:A, 0:A]), (p1[:, :], bk[7][0:A, A:A + D])),
                                 ((fm[:, :], bk[7][0:A, 0:D]),),
                                 ((M[:, :], bk[7][:, 0:D]),))[n - 1]:
                    last = act.activation(dst, src, ACT.Copy)
                last.then_inc(s["post_cp"], 1)

            act.wait_ge(s["ld_prm"], 16)
            act.wait_ge(s["bi_done"], 1)
            for w in range(SLOTS):
                if POST + 1 < w <= POST + 6:
                    copies(w - POST - 1)
                if w + 1 < W:
                    stage(w + 1)
                if w < W:
                    after(act, "mm2_done", w - 1)
                    for c in range(IC):
                        if c % 2 == 0:
                            act.wait_ge(s["mm1_done"], 2 * w + c // 2 + 1)
                        act.activation(hT[:, w % 2, c * NP:(c + 1) * NP], H[w % 2][c // 2][:, (c % 2) * NP:(c % 2 + 1) * NP],
                                       ACT.Gelu, bias=biW[:, c, w:w + 1]).then_inc(s["gelu_done"], 1)
                if w == POST + 7:
                    act.activation(saf[:, 1, :], safety, ACT.Tanh, scale=0.5).then_inc(s["saf_a"], 1)
            all_y1_stored(act)
            load_x1(act, range(1))
            act.wait_ge(s["hb2_done"], 1)
            act.wait_ge(s["eobd_zero"], 1)

            def gate_h1(k):
                act.wait_ge(s["h1_mm"], k + 1)
                after(act, "st_mm", k - 1)
                act.activation(h1[:, k % 2, :], bk[7][0:R, 0:GPQ * Q], ACT.Relu, bias=gb1[:, :],
                               scale=1.0 / S).then_inc(s["h1_done"], 1)

            def gate_tanh(k):
                act.wait_ge(s["st_mm"], k + 1)
                after(act, "st_done", k)
                act.activation(stg[:, 0, :], bk[7][:, 64:64 + GPQ], ACT.Tanh, bias=hb2[:, :], scale=0.5)\
                   .then_inc(s["tanh_done"], 1)

            def spread(i):
                act.wait_ge(s["eo_mm"], i + 1)
                after(act, "up_done", i)
                for q in range(Q):
                    last = act.activation(eobd[A * q:A * q + A, :, q, :], blocks(q), ACT.Copy)
                last.then_inc(s["eobd_done"], 1)

            def x1_T(i):
                act.wait_ge(s["xp_done"], i + 1)
                after(act, "down_done", i - 1)
                act.activation(x1T[:, i % 2, :], bk[6][:, :], ACT.Copy).then_inc(s["x1T_done"], 1)

            def hidden(i):
                act.wait_ge(s["down_done"], i + 1)
                after(act, "eo_mm", i - 1)
                act.activation(hid[:, i % 2, :], bk[0][:, 0:GPQ * S], ACT.Gelu, bias=db4[:, :]).then_inc(s["hid_done"], 1)

            def normalize(k):
                p = k % 2
                act.wait_ge(s["nmr2_done"], k + 1)
                act.wait_ge(s["r2_done"], k + 1)
                after(act, "y2T_done", k - 1)
                after(act, "x2k_a", k - 1)
                for g in range(GPQ):
                    last = act.activation(y2[:, p, g * D:(g + 1) * D], r2[:, p, g * D:(g + 1) * D], ACT.Identity,
                                          scale=ln2s[:, p, 1, g:g + 1], bias=ln2s[:, p, 3, g:g + 1])
                last.then_inc(s["y2_done"], 1)

            def x2_T(k):
                p = k % 2
                act.wait_ge(s["y2T_done"], k + 1)
                after(act, "z_done3", k - 1)
                after(act, "pool_done", k - 1)
                act.activation(x2T[:, p, :], bk[4][:, :], ACT.Identity, scale=lnc[:, 0:1], bias=lnc[:, 1:2])\
                   .then_inc(s["x2T_done"], 1)

            for t in range(-2, NQ + 4):
                if 0 <= t < NQ:
                    spread(t)
                if 0 <= t - 4 < NQ:
                    gate_tanh(t - 4)
                if 0 <= t + 1 < NQ:
                    hidden(t + 1)
                if 0 <= t + 2 < NQ:
                    x1_T(t + 2)
                if 0 <= t - 2 < NQ:
                    x2_T(t - 2)
                if 0 <= t - 3 < NQ:
                    gate_h1(t - 3)
                if 0 <= t - 1 < NQ:
                    normalize(t - 1)

        @block.vector
        def _(dve):
            def split3(k, full, rest, parts):
                dve.tensor_copy(parts[:, 0, :], full).then_inc(s["rsp_a"], 1)
                dve.wait_ge(s["rsp_a"], k + 1)
                dve.tensor_tensor(rest[:, 0, :], full, parts[:, 0, :], ALU.subtract).then_inc(s["rsp_b"], 1)
                dve.wait_ge(s["rsp_b"], k + 1)
                dve.tensor_copy(parts[:, 1, :], rest[:, 0, :]).then_inc(s["rsp_c"], 1)
                dve.wait_ge(s["rsp_c"], k + 1)
                dve.tensor_tensor(rest[:, 1, :], rest[:, 0, :], parts[:, 1, :], ALU.subtract).then_inc(s["rsp_d"], 1)
                dve.wait_ge(s["rsp_d"], k + 1)
                dve.tensor_copy(parts[:, 2, :], rest[:, 1, :]).then_inc(s["rsp_done"], 1)

            dve.wait_ge(s["ld_ang"], 16)
            dve.tensor_scalar(ang[:, 2:4], ang[:, 0:2], 1.0 / (TWO_PI_HI + TWO_PI_LO), MAGIC, ALU.mult, ALU.add)\
               .then_inc(s["ang_a"], 1)
            dve.wait_ge(s["ang_a"], 1)
            dve.tensor_scalar(ang[:, 8:10], ang[:, 2:4], -MAGIC, None, ALU.add).then_inc(s["ang_b"], 1)
            dve.wait_ge(s["ang_b"], 1)
            dve.scalar_tensor_tensor(ang[:, 2:4], ang[:, 8:10], -TWO_PI_HI, ang[:, 0:2], ALU.mult, ALU.add)\
               .then_inc(s["ang_c"], 1)
            dve.wait_ge(s["ang_c"], 1)
            dve.scalar_tensor_tensor(ang[:, 4:6], ang[:, 8:10], -TWO_PI_LO, ang[:, 2:4], ALU.mult, ALU.add)\
               .then_inc(s["ang_d"], 1)
            dve.wait_ge(s["ang_d"], 1)
            dve.scalar_tensor_tensor(ang[:, 2:4], ang[:, 4:6], -1.0, ang[:, 4:6], ALU.mult, ALU.min).then_inc(s["ang_d"], 1)
            dve.wait_ge(s["ang_d"], 2)
            dve.tensor_scalar(ang[:, 6:8], ang[:, 2:4], float(3.14159265358979 / 2), None, ALU.add).then_inc(s["ang_e"], 1)
            dve.wait_ge(s["ld_ids"], 32)
            dve.tensor_copy(e1c[:, :], e1c_i[:, :])
            dve.tensor_copy(e1r[:, :], e1r_i[:, :]).then_inc(s["ids_f"], 1)
            dve.wait_ge(s["ld_const"], 16)
            dve.wait_ge(s["ids_f"], 1)
            dve.tensor_scalar(oh1r[:, :], e1r[:, :], const("part3", E3), None, ALU.is_equal).then_inc(s["oh1r_done"], 1)
            dve.tensor_scalar(oh1[:, :], const("expert"), e1c[:, :], None, ALU.is_equal).then_inc(s["oh1_done"], 1)
            dve.wait_ge(s["oh1r_done"], 1)
            dve.reduce_sum(cnt[:, 0:1], oh1r[:, :], axis=AX.X).then_inc(s["cnt_done"], 1)
            dve.wait_ge(s["cnt_done"], 1)
            dve.tensor_scalar(cnt[:, 3:4], cnt[:, 0:1], 1.0 / Q, (Q - 1) / Q - (Q - 1) / (2 * Q), ALU.mult, ALU.add)\
               .then_inc(s["wcount_a"], 1)
            dve.wait_ge(s["wcount_a"], 1)
            dve.tensor_scalar(cnt[:, 1:2], cnt[:, 3:4], MAGIC, -MAGIC, ALU.add, ALU.add).then_inc(s["wcount_done"], 1)
            dve.wait_ge(s["rank_mm"], 1)
            dve.tensor_tensor_reduce(out=rank[:, 0:E1], in0=bk[5][:, 0:E1], in1=oh1[:, :], scale=1.0, scalar=0.0,
                                     op0=ALU.mult, op1=ALU.add, accum_out=ang[:, 0:1]).then_inc(s["rank_done"], 1)
            dve.wait_ge(s["start_mm"], 1)
            dve.tensor_copy(cnt[:, 2:3], bk[4][0:E3, 500:501])
            dve.tensor_scalar(start4[:, :], bk[4][0:E3, 500:501], float(Q), None, ALU.mult).then_inc(s["start_done"], 1)
            dve.wait_ge(s["start_done"], 1)
            dve.tensor_tensor(cnt[:, 3:4], cnt[:, 2:3], cnt[:, 1:2], ALU.add).then_inc(s["end_done"], 1)
            dve.wait_ge(s["base_mm"], 1)
            dve.wait_ge(s["rank_done"], 1)
            dve.tensor_copy(ang[:, 1:2], bk[6][:, 0:1]).then_inc(s["base_done"], 1)
            dve.wait_ge(s["base_done"], 1)
            dve.tensor_scalar(place[:, :], const("slots"), ang[:, 0:1], ang[:, 1:2], ALU.subtract, ALU.is_equal)\
               .then_inc(s["place_done"], 1)
            dve.wait_ge(s["place_done"], 1)
            dve.scalar_tensor_tensor(placed[:, :], const("slots"), const("fromend"), place[:, :], ALU.add, ALU.mult)\
               .then_inc(s["placed_done"], 1)
            dve.tensor_scalar(ohw[:, 0, :], const("windows", E3), cnt[:, 2:3], None, ALU.is_ge)
            dve.wait_ge(s["end_done"], 1)
            dve.tensor_scalar(ohw[:, 1, :], const("windows", E3), cnt[:, 3:4], None, ALU.is_lt).then_inc(s["ohw_a"], 1)
            dve.wait_ge(s["ohw_a"], 1)
            dve.tensor_tensor(ohw[:, 0, :], ohw[:, 0, :], ohw[:, 1, :], ALU.mult).then_inc(s["ohw_done"], 1)
            dve.wait_ge(s["trig_done"], 1)
            dve.tensor_scalar(ang[:, 6:8], ang[:, 8:10], -1.0, None, ALU.mult).then_inc(s["nst_done"], 1)
            dve.wait_ge(s["nst_done"], 1)

            def perm_copy(k):
                dve.wait_ge(s["perm_mm"], k + 1)
                m = min(PS, S - k * PS)
                dve.tensor_copy(xT[:, :, k * PS:k * PS + m, :],
                                bk[k % 4][:, 0:m * NSLOT].rearrange("p (s w q) -> p w s q", s=m, q=Q)).then_inc(s["perm_dve"], 1)

            for k in range(NX):
                dve.wait_ge(s["rot_a"], k + 1)
                r = slice(k * SC, (k + 1) * SC)
                for o, i_, c in ((0, 1, 8), (1, 0, 6), (2, 3, 9), (3, 2, 7)):
                    last = dve.scalar_tensor_tensor(quad[:, r, :, o], quad_in[:, r, :, i_], ang[:, c:c + 1],
                                                    quad[:, r, :, o], ALU.mult, ALU.add)
                last.then_inc(s["rot_done"], 1)
                if k == 1:
                    dve.wait_ge(s["ew_mm"], 1)
                    dve.tensor_copy(ew_i[:, :], bk[5][0:1, 0:WP]).then_inc(s["ew_done"], 1)
                if k == 3:
                    dve.wait_ge(s["pl_mm"], 1)
                    dve.tensor_copy(pl_row[:, :], bk[6][0:1, 256:256 + NSLOT]).then_inc(s["pl_done"], 1)
            for k in range(1, NPERM, 2):
                perm_copy(k)
                if k == 3:
                    dve.wait_ge(s["gram_mm"], 1)
                    dve.tensor_copy(Z[:, 0:A], bk[7][0:2 * A, 0:A])
                    dve.tensor_copy(Z[:, A:2 * A], const("eye32", 2 * A)).then_inc(s["z_done"], 1)
                if k == 5:
                    dve.tensor_copy(oh16[:, :], ohw[:, 0, :]).then_inc(s["oh16_done"], 1)
                    split3(0, param("l1_bo"), bo_rest, bo3)
                    dve.wait_ge(s["rsp_done"], 1)
                    dve.tensor_scalar(bo24[:, 0, :], bo3[:, 0, :], const("third", E3)[:, 0:1], None, ALU.mult)\
                       .then_inc(s["bo24_done"], 1)
                    for k in (1, 2):
                        dve.wait_ge(s["bo24_done"], k)
                        dve.scalar_tensor_tensor(bo24[:, k, :], bo3[:, k, :], const("third", E3)[:, k:k + 1],
                                                 bo24[:, k - 1, :], ALU.mult, ALU.add).then_inc(s["bo24_done"], 1)
                if k == 9:
                    dve.wait_ge(s["row_mm"], 1)
                    dve.tensor_tensor(row_i[:, :], bk[6][:, 0:W], const("rowbase"), ALU.add)\
                       .then_inc(s["row_done"], 1)

            dve.wait_ge(s["ew_done"], 1)
            dve_load, dve_expert = expert_regs(dve, "dve")
            keep, rot = [0] * A, [(k + 1) % A for k in range(A)]

            def of_expert(w, k):
                return vec[:, bass.ds(dve_expert(w), 1), k, :].rearrange("p o d -> p (o d)")

            for w in range(SLOTS):
                j, v, u = w, w - 2, w - 3
                gs = j < A
                if 0 <= v < W:
                    dve_load(v)
                    dve.wait_ge(s["mm2_done"], v + 1)
                    dve.bn_stats(bst[:, :], OT[v % 3][:, 0:NP]).then_inc(s["bst_done"], 1)
                if gs:
                    dve.wait_ge(s["z_done"], j + 1)
                    dve.stream_shuffle(Zp[:, :], Z[:, :], keep).then_inc(s["piv_done"], 1)
                    dve.stream_shuffle(Zs[:, :], Z[:, :], rot).then_inc(s["zs_done"], 1)
                if 0 <= u < W:
                    dve.wait_ge(s["rstd_done"], u + 1)
                    dve.scalar_tensor_tensor(y1[:, u % NY, :], yg[:, :], rstd[:, u % 2:u % 2 + 1], of_expert(u, 1),
                                             ALU.mult, ALU.add).then_inc(s["y1_done"], 1)
                if gs:
                    dve.wait_ge(s["zs_done"], j + 1)
                    a0 = c_at["lastrow"][0]
                    dve.tensor_tensor(gsv[:, 1:2], Zs[:, j:j + 1], cst[0:2 * A, a0 + j:a0 + j + 1], ALU.mult)\
                       .then_inc(s["t0_done"], 1)
                if 0 <= v < W:
                    dve.wait_ge(s["bst_done"], v + 1)
                    dve.bn_aggr(mv[:, v % 2, :], bst[:, :]).then_inc(s["mv_done"], 1)
                if gs:
                    dve.wait_ge(s["gpow_done"], j + 1)
                    dve.tensor_scalar(gsv[:, 2:3], gsv[:, 0:1], EPS3, None, ALU.add).then_inc(s["gadd_done"], 1)
                if v == 0:
                    dve.wait_ge(s["ld_vec"], 16)
                if 0 <= v < W:
                    dve.wait_ge(s["mv_done"], v + 1)
                    dve.scalar_tensor_tensor(yg[:, :], OT[v % 3][:, 0:NP], mv[:, v % 2, 0:1], of_expert(v, 0),
                                             ALU.subtract, ALU.mult).then_inc(s["yg_done"], 1)
                if gs:
                    dve.wait_ge(s["gadd_done"], j + 1)
                    dve.reciprocal(gsv[:, 3:4], gsv[:, 2:3]).then_inc(s["grec_done"], 1)
                if 0 <= v < W:
                    dve.tensor_scalar(ve[:, v % 2:v % 2 + 1], mv[:, v % 2, 1:2], EPS1, None, ALU.add)\
                       .then_inc(s["ve_done"], 1)
                if gs:
                    dve.wait_ge(s["grec_done"], j + 1)
                    dve.tensor_scalar(gsv[:, 4:5], gsv[:, 1:2], gsv[:, 3:4], gsv[:, 3:4], ALU.mult, ALU.mult)\
                       .then_inc(s["t_done"], 1)
                    dve.wait_ge(s["t_done"], j + 1)
                    dve.scalar_tensor_tensor(Z[:, :], Zp[:, :], gsv[:, 4:5], Zs[:, :], ALU.mult, ALU.add)\
                       .then_inc(s["z_done"], 1)
                if w == 1:
                    dve.wait_ge(s["ld_ids2"], 32)
                    dve.tensor_copy(e2f[:, :], e2c_i[:, :])
                    dve.tensor_copy(e2r[:, :], e2r_i[:, :]).then_inc(s["e2f_a"], 1)
                    dve.wait_ge(s["e2f_a"], 1)
                    dve.tensor_scalar(e2f[:, :], e2f[:, :], 1.0, 0.0, ALU.add, ALU.max)
                    dve.tensor_scalar(e2r[:, :], e2r[:, :], 1.0, 0.0, ALU.add, ALU.max).then_inc(s["e2f_done"], 1)
                    dve.wait_ge(s["e2f_done"], 1)
                    dve.tensor_scalar(e2g_i[:, :], e2f[:, :], float(E2 - 1), None, ALU.min).then_inc(s["e2g_done"], 1)
                    dve.tensor_scalar(oh2r[:, :], e2r[:, :], float(E2 - 1), const("part", E2), ALU.min, ALU.is_equal)\
                       .then_inc(s["oh2r_done"], 1)
                if w == A:
                    dve.wait_ge(s["bias_mm"], 1)
                    dve.tensor_copy(brow[:, :], bk[7][0:B // Q, 64:64 + NP]).then_inc(s["bias_done"], 1)
                if w == POST - 1:
                    dve.wait_ge(s["z_done"], A + 1)
                    dve.tensor_tensor_reduce(out=Zp[:, 0:A], in0=Z[:, 0:A], in1=const("eye32", 2 * A), scale=1.0,
                                             scalar=0.0, op0=ALU.mult, op1=ALU.add, accum_out=gsv[:, 5:6])\
                       .then_inc(s["diag_done"], 1)
                if w == POST:
                    dve.wait_ge(s["dpow_done"], 1)
                    dve.tensor_scalar(gsv[:, 7:8], gsv[:, 6:7], EPS3, None, ALU.add).then_inc(s["dadd_done"], 1)
                    dve.wait_ge(s["dadd_done"], 1)
                    dve.reciprocal(gsv[:, 6:7], gsv[:, 7:8]).then_inc(s["drec_done"], 1)
                    dve.wait_ge(s["drec_done"], 1)
                    dve.tensor_scalar(Zs[:, 0:A], Z[:, A:2 * A], gsv[:, 6:7], None, ALU.mult).then_inc(s["ts_done"], 1)
            dve.tensor_copy(in_group[:, :, :], const("in_group", 3 * GPQ).rearrange("p (g o) -> p g o", o=1)
                            .broadcast_to([3 * GPQ, GPQ, S])).then_inc(s["in_group_done"], 1)
            dve.wait_ge(s["bias_done"], 1)
            split3(1, brow[:, :], brest, bparts)
            dve.wait_ge(s["ld_rows"], 16 * 2)
            split3(2, rrow[:, 2, :], rrow[:, 3:5, :], rsp[:, 0, :, :])
            dve.tensor_tensor(rrow[:, 5, :], rrow[:, 0, :], rrow[:, 1, :], ALU.add).then_inc(s["rrow_a"], 1)
            dve.wait_ge(s["rrow_a"], 1)
            split3(3, rrow[:, 5, :], rrow[:, 6:8, :], rsp[:, 1, :, :])
            dve.tensor_scalar(hb2[:, :], gb2[:, :], 0.5, None, ALU.mult).then_inc(s["hb2_done"], 1)
            dve.wait_ge(s["saf_a"], 1)
            dve.tensor_scalar(saf[:, 0, :], saf[:, 1, :], 0.25 * KNOB, 0.25 * KNOB, ALU.mult, ALU.add).then_inc(s["saf_done"], 1)
            dve.wait_ge(s["saf_done"], 1)

            def pool_sum(k):
                p = k % 2
                dve.wait_ge(s["x2T_done"], k + 1)
                after(dve, "h1_mm", k - 1)
                dve.reduce_sum(pooled[:, p, :], x2T[:, p, :].rearrange("p (b s) -> p b s", s=S), axis=AX.X)\
                   .then_inc(s["pool_done"], 1)

            def strengths(k):
                p = k % 2
                dve.wait_ge(s["tanh_done"], k + 1)
                dve.scalar_tensor_tensor(stt_[:, p, :], stg[:, 0, :], 1.0, saf[:, 0, GPQ * k:GPQ * (k + 1)], ALU.add,
                                         ALU.mult).then_inc(s["st_done"], 1)

            def finish(k):
                p = k % 2
                dve.wait_ge(s["st_done"], k + 1)
                dve.wait_ge(s["z_done3"], k + 1)
                dve.wait_ge(s["x2k_done"], k + 1)
                after(dve, "out_done", 16 * (k - 1))
                for g in range(GPQ):
                    last = dve.scalar_tensor_tensor(oS[:, p, g, :], Z3[k % 2][:, g * D:(g + 1) * D], stt_[:, p, g:g + 1],
                                                    x2k[:, k % NK, g * D:(g + 1) * D], ALU.mult, ALU.add)
                last.then_inc(s["o_done"], 1)

            def residual(i):
                p = i % 2
                dve.wait_ge(s["up_done"], i + 1)
                dve.wait_ge(s[f"ld_x1_{i}"], 16)
                after(dve, "y2_done", i - 1)
                after(dve, "mv2_done", i)
                dve.tensor_tensor(r2[:, p, :], bk[2][:, :], x1k[:, i, :], ALU.add).then_inc(s["r2_done"], 1)

            def statistics(i):
                p = i % 2
                dve.wait_ge(s["r2_done"], i + 1)
                for g in range(GPQ):
                    dve.bn_stats(bst2[:, g, :], r2[:, p, g * D:(g + 1) * D]).then_inc(s["bst2_done"], 1)
                after(dve, "nmean2_done", i - 1)
                for g in range(GPQ):
                    dve.wait_ge(s["bst2_done"], GPQ * i + g + 1)
                    last = dve.bn_aggr(mv2[:, p, g, :], bst2[:, g, :])
                last.then_inc(s["mv2_done"], 1)

            def variance(i):
                p = i % 2
                dve.wait_ge(s["mv2_done"], i + 1)
                dve.tensor_scalar(ln2s[:, p, 0, :], mv2[:, p, :, 1], EPS2, None, ALU.add).then_inc(s["ve2_done"], 1)
                dve.tensor_scalar(ln2s[:, p, 2, :], mv2[:, p, :, 0], -1.0, None, ALU.mult).then_inc(s["nmean2_done"], 1)

            for t in range(NQ + 4):
                if 0 <= t - 3 < NQ:
                    pool_sum(t - 3)
                if 0 <= t - 4 < NQ:
                    strengths(t - 4)
                if 0 <= t - 4 < NQ:
                    finish(t - 4)
                if 0 <= t < NQ:
                    residual(t)
                if 0 <= t < NQ:
                    statistics(t)
                if 0 <= t < NQ:
                    variance(t)

        @block.tensor
        def _(pe):
            mm = pe.matmul

            def keep_warm(n):
                for _ in range(n):
                    mm(bk[2][:, :], zeros[:, 0:NP], zeros[:, :], start=True, stop=True)

            pe.wait_ge(s["zeros_done"], 1)
            keep_warm(3)
            pe.wait_ge(s["oh1_done"], 1)
            mm(bk[5][:, 0:E1], const("before"), oh1[:, :], start=True, stop=True).then_inc(s["rank_mm"], 1)
            pe.wait_ge(s["wcount_done"], 1)
            mm(bk[4][0:E3, 500:501], const("before8", E1), cnt[0:E1, 1:2], start=True, stop=True).then_inc(s["start_mm"], 1)
            pe.wait_ge(s["start_done"], 1)
            mm(bk[6][:, 0:1], oh1r[0:E1, :], start4[0:E1, :], start=True, stop=True).then_inc(s["base_mm"], 1)
            keep_warm(1)
            pe.wait_ge(s["ohw_done"], 1)
            pe.wait_ge(s["rank_done"], 1)
            mm(bk[5][0:1, 0:WP], const("part", E1), ohw[0:E1, 0, :], start=True, stop=True).then_inc(s["ew_mm"], 1)
            keep_warm(1)
            pe.wait_ge(s["place_done"], 1)
            for k in range(NPERM):
                for t in range(k * PS, min(S, (k + 1) * PS)):
                    if t % SC == 0:
                        pe.wait_ge(s["rot_done"], t // SC + 1)
                    if t == k * PS and k >= 4:
                        pe.wait_ge(s["perm_act" if k % 2 == 0 else "perm_dve"], k // 2 - 1)
                    last = mm(bk[k % 4][:, (t - k * PS) * NSLOT:(t - k * PS + 1) * NSLOT], xr[:, t, :], place[:, :],
                              start=True, stop=True)
                last.then_inc(s["perm_mm"], 1)
                if k == 1:
                    pe.wait_ge(s["placed_done"], 1)
                    mm(bk[6][0:1, 256:256 + NSLOT], const("ones"), placed[:, :], start=True, stop=True)\
                        .then_inc(s["pl_mm"], 1)
                if k == 3:
                    pe.wait_ge(s["ld_prm"], 16)
                    for m in range(2):
                        last = mm(bk[7][A * m:A * m + A, 0:A], uv_s[:, m * A:(m + 1) * A], uv_s[:, m * A:(m + 1) * A], start=True, stop=True)
                    last.then_inc(s["gram_mm"], 1)
                    for c in range(IC):
                        last = mm(bk[4][:, c * W:(c + 1) * W], bi_s[:, c * D:(c + 1) * D], ohw[0:E1, 0, 0:W], start=True, stop=True)
                    last.then_inc(s["bi_mm"], 1)
                if k == 7:
                    pe.wait_ge(s["pl_done"], 1)
                    pe.wait_ge(s["ld_mask"], 16)
                    for q in range(Q):
                        last = mm(bk[6][:, 0:W], mask[:, q * NP:(q + 1) * NP],
                                  pl_row[:, :].rearrange("o (w q) -> o w q", q=Q)[:, :, q], start=(q == 0),
                                  stop=(q == Q - 1))
                    last.then_inc(s["row_mm"], 1)
            pe.wait_ge(s["perm_act"], (NPERM + 1) // 2)
            pe.wait_ge(s["perm_dve"], NPERM // 2)
            pe.wait_ge(s["bi_done"], 1)
            pe.wait_ge(s["ew_done"], 1)
            pe.wait_ge(s["oh16_done"], 1)
            pe.wait_ge(s["bo24_done"], 3)
            pe_load, pe_expert = expert_regs(pe, "pe")

            def up_to_tokens(w):
                pe_load(w)
                e = pe_expert(w)
                after(pe, "yg_done", w - 2)
                mm(OT[w % 3][:, 0:NP], oh16[:, w:w + 1].broadcast_to([E3, NP]), bo24[:, 2, :], start=True, stop=False)
                mm(OT[w % 3][:, 0:NP], xT[:, w, :, :].rearrange("p s q -> p (s q)"), ident, start=False, stop=False)
                for c in range(IC):
                    pe.wait_ge(s["gelu_done"], w * IC + c + 1)
                    last = mm(OT[w % 3][:, 0:NP], hT[:, w % 2, c * NP:(c + 1) * NP],
                              bank[:, 1, bass.ds(e, 1), c * D:(c + 1) * D].rearrange("p o d -> p (o d)"),
                              start=False, stop=(c == IC - 1))
                last.then_inc(s["mm2_done"], 1)

            def post(n):
                t7 = bk[7]
                if n == 1:
                    pe.wait_ge(s["ts_done"], 1)
                    last = pe.transpose(t7[0:A, 0:2 * A], Zs[:, 0:A], cst[0:2 * A, 0:2 * A])
                elif n == 2:
                    pe.wait_ge(s["post_cp"], 1)
                    mm(t7[0:A, 0:D], tt_s[:, 0, :], uvt_s[:, 0:D], start=True, stop=True)
                    mm(t7[0:A, D:D + A], uvt_s[:, 0:A], tt_s[:, 0, :], start=True, stop=True)
                    last = mm(t7[:, D + A:D + 2 * A], uvt_s[:, D:2 * D], tt_s[:, 1, :], start=True, stop=True)
                elif n == 3:
                    pe.wait_ge(s["post_cp"], 2)
                    mm(t7[0:A, 0:A], vo[:, :], vo[:, :], start=True, stop=True)
                    last = mm(t7[0:A, A:A + D], ur[:, :], rwt[:, :], start=True, stop=True)
                elif n == 4:
                    pe.wait_ge(s["post_cp"], 3)
                    last = mm(t7[0:A, 0:D], vv[:, :], p1[:, :], start=True, stop=True)
                else:
                    pe.wait_ge(s["post_cp"], 4)
                    last = mm(t7[:, 0:D], uo_t[:, :], fm[:, :], start=True, stop=True)
                last.then_inc(s["post_pe"], 1)

            for w in range(SLOTS):
                if w < W:
                    pe.wait_ge(s["wi_staged"], w + 1)
                    for c in range(IC):
                        if c % 2 == 0:
                            after(pe, "gelu_done", (w - 2) * IC + c + 2)
                        last = mm(H[w % 2][c // 2][:, (c % 2) * NP:(c % 2 + 1) * NP], wi_st[:, w % 2, c * D:(c + 1) * D],
                                  xT[:, w, :, :].rearrange("p s q -> p (s q)"), start=True, stop=True)
                        if c % 2 == 1:
                            last.then_inc(s["mm1_done"], 1)
                if w == 1:
                    pe.wait_ge(s["ld_wo"], 16)
                if 0 <= w - 1 < W:
                    up_to_tokens(w - 1)
                if w == 2:
                    pe.wait_ge(s["oh2r_done"], 1)
                    pe.wait_ge(s["z_done"], 1)
                    for q in range(Q):
                        cols = slice(64 + A * q, 64 + A * q + A)
                        mm(bk[7][0:B // Q, cols], oh2r[:, q:B:Q], dbt[:, :], start=True, stop=False)
                        last = mm(bk[7][0:B // Q, cols], oh2r[:, q:B:Q], det[:, :], start=False, stop=True)
                    last.then_inc(s["bias_mm"], 1)
                if POST < w <= POST + 5:
                    post(w - POST)
            def load_T(i):
                pe.wait_ge(s[f"ld_x1_{i}"], 16)
                after(pe, "x1T_done", i)
                for g in range(GPQ):
                    last = pe.transpose(bk[6][:, g * D:(g + 1) * D], x1k[:, i, g * D:(g + 1) * D], ident)
                last.then_inc(s["xp_done"], 1)

            def down(i):
                pe.wait_ge(s["x1T_done"], i + 1)
                after(pe, "hid_done", i)
                v = x1T[:, i % 2, :].rearrange("p (g q s) -> p g q s", g=GPQ, q=Q)
                for q in range(Q):
                    last = mm(bk[0][A * q:A * q + A, 0:GPQ * S], dwt[:, :], v[:, :, q, :], start=True, stop=True)
                last.then_inc(s["down_done"], 1)

            def expert(i):
                if i == 0:
                    pe.wait_ge(s["dW_done"], 16 * Q)
                    pe.wait_ge(s["brow3_done"], 16)
                    pe.wait_ge(s["in_group_done"], 1)
                pe.wait_ge(s["hid_done"], i + 1)
                after(pe, "eobd_done", i)
                mm(bk[1][:, 0:GPQ * S], brow3[:, i, :], in_group[:, :, :].rearrange("k g s -> k (g s)"), start=True, stop=False)
                for g in range(GPQ):
                    last = mm(bk[1][:, g * S:(g + 1) * S], dW[:, GPQ * i + g, :, :].rearrange("p q o -> p (q o)"),
                              hid[:, i % 2, g * S:(g + 1) * S], start=False, stop=(g == GPQ - 1))
                last.then_inc(s["eo_mm"], 1)

            def bias(bank_, k):
                mm(bank_[:, :], ones3[:, :], rb3[:, k, :].rearrange("k (o d) -> k o d", o=1).broadcast_to([3, GPQ, D]),
                   start=True, stop=False)

            def up(i):
                if i == 0:
                    pe.wait_ge(s["rb3_done"], 16 * 6)
                after(pe, "r2_done", i)
                bias(bk[2], 0)
                pe.wait_ge(s["eobd_done"], i + 1)
                for g in range(GPQ):
                    last = mm(bk[2][:, g * D:(g + 1) * D], eobd[:, g, :, :].rearrange("p q s -> p (q s)"), ut4[:, :],
                              start=False, stop=(g == GPQ - 1))
                last.then_inc(s["up_done"], 1)

            def back(i):
                pe.wait_ge(s["y2_done"], i + 1)
                after(pe, "x2T_done", i)
                for g in range(GPQ):
                    last = pe.transpose(bk[4][:, g * D:(g + 1) * D], y2[:, i % 2, g * D:(g + 1) * D], ident)
                last.then_inc(s["y2T_done"], 1)

            def gate(i):
                pe.wait_ge(s["pool_done"], i + 1)
                after(pe, "tanh_done", i)
                mm(bk[7][0:R, 0:GPQ * Q], gw1[:, :], pooled[:, i % 2, :], start=True, stop=True).then_inc(s["h1_mm"], 1)

            def response(i):
                if i == 0:
                    pe.wait_ge(s["post_cp"], 5)
                pe.wait_ge(s["x2T_done"], i + 1)
                after(pe, "o_done", i - 1)
                bias(Z3[i % 2], 1)
                for g in range(GPQ):
                    last = mm(Z3[i % 2][:, g * D:(g + 1) * D], x2T[:, i % 2, g * D:(g + 1) * D], M[:, :], start=False,
                              stop=(g == GPQ - 1))
                last.then_inc(s["z_done3"], 1)

            def strength(i):
                pe.wait_ge(s["h1_done"], i + 1)
                for q in range(Q):
                    last = mm(bk[7][S * q:S * q + S, 64:64 + GPQ], gw2[:, 0:1].broadcast_to([R, S]),
                              h1[:, i % 2, q:GPQ * Q:Q], start=True, stop=True)
                last.then_inc(s["st_mm"], 1)

            keep_warm(11)
            for t in range(-2, NQ + 4):
                if 0 <= t < NQ:
                    expert(t)
                if 0 <= t + 1 < NQ:
                    down(t + 1)
                if 0 <= t + 2 < NQ:
                    load_T(t + 2)
                if 0 <= t - 4 < NQ:
                    strength(t - 4)
                if 0 <= t - 2 < NQ:
                    back(t - 2)
                if 0 <= t < NQ:
                    up(t)
                if 0 <= t - 3 < NQ:
                    gate(t - 3)
                if 0 <= t - 3 < NQ:
                    response(t - 3)


def kernel(**inputs):
    import numpy as np
    import concourse.bacc as bacc
    from concourse import mybir
    from concourse.bass_utils import run_bass_kernel_spmd

    a = {k: np.asarray(v) for k, v in inputs.items()}
    f = np.float32
    B, S, D = a["x"].shape
    E1, E2 = a["L1_cond_Wi"].shape[0], a["L2_cond_expert_W"].shape[0]
    A = a["L2_cond_down_W"].shape[0]
    Q = 4
    W = (B + E1 * (Q - 1)) // Q
    NSLOT = W * Q
    p = np.arange(128)
    lastrow = np.where((p[:, None] % A) <= A - 2 - np.arange(A)[None], -1.0, 0.0)
    WP = -(-W // 4) * 4
    tokmask = np.concatenate([-S * (p[None] % Q == q) for q in range(Q)], axis=1).astype(f)
    rowbase = S * (B + Q * np.arange(W)[None] + p[:, None] % Q) + p[:, None] // Q
    const = np.concatenate([
        np.eye(128), (p[:, None] < p[None, :]), np.tile(np.arange(NSLOT), (128, 1)), np.tile(np.arange(E1), (128, 1)),
        p[:, None], lastrow, np.eye(A)[p % A], (p[:, None] < np.arange(3 * E1)[None] % E1),
        p[:, None] % E1, p[:, None] // E1 == np.arange(3)[None],
        p[:, None] // 3 == np.arange(4)[None],
        np.tile(np.arange(WP), (128, 1)), B - p[:, None], rowbase, np.ones((128, 1))],
        axis=1).astype(f)
    eye = np.eye(A, dtype=f).reshape(1, A * A)
    wt = a["L2_cond_expert_W"].transpose(0, 2, 1).reshape(E2, A * A)
    zero = np.zeros((1, A), f)
    emb = a["L2_cond_domain_emb"]
    l1_w = np.stack([a["L1_cond_Wi"].transpose(1, 0, 2),
                     a["L1_cond_Wo"].reshape(E1, -1, 128, D).transpose(2, 0, 1, 3).reshape(128, E1, -1)], axis=1)
    l1_vec = np.stack([a["L1_cond_gamma"], a["L1_cond_beta"]], axis=1)
    parts = {
        "uv": np.concatenate([a["L3_cond_U"], a["L3_cond_V"]], axis=1),
        "uv_t": np.concatenate([a["L3_cond_U"].T, a["L3_cond_V"].T], axis=1),
        "l1_bi": a["L1_cond_bi"], "l1_bo": np.tile(a["L1_cond_bo"], (3, 1)),
        "down_wt": a["L2_cond_down_W"].T, "down_b4": np.tile(a["L2_cond_down_b"], Q).reshape(Q * A, 1),
        "up_t4": np.tile(a["L2_cond_up_W"].T, (Q, 1)),
        "dom_b": np.concatenate([zero, a["L2_cond_expert_b"], zero]),
        "dom_e": np.concatenate([emb[:1], emb, emb[-1:]]),
        "ln_cols": np.stack([a["L2_cond_ln_gamma"], a["L2_cond_ln_beta"]], axis=1),
        "gate_w1t": a["L3_cond_gate_w1"].T, "gate_b1": a["L3_cond_gate_b1"].reshape(-1, 1),
        "gate_w2": a["L3_cond_gate_w2"].reshape(-1, 1), "gate_b2": np.tile(a["L3_cond_gate_b2"].reshape(1, 1), (128, 1)),
        "resp_wt": a["L3_cond_resp_w"].T,
        "safety": np.repeat(a["condB_safetyscore"].reshape(B // Q, Q).T, S, axis=0),
    }
    param_at, params, n = {}, [], 0
    for name, v in parts.items():
        param_at[name] = (v.shape[0], n, v.shape[1])
        params.append(np.pad(v, ((0, 128 - v.shape[0]), (0, 0))))
        n += v.shape[1]
    ins = {
        "x": a["x"],
        "expert1_col": a["itok_B_0_7"].reshape(B, 1), "expert1_row": a["itok_B_0_7"],
        "expert2_col": a["itok_B_0_15"].reshape(B, 1), "expert2_row": a["itok_B_0_15"],
        "angles": np.stack([a["condB_theta"], a["condB_phi"]], axis=1),
        "l1_w": l1_w, "l1_vec": l1_vec,
        "dom_w": np.concatenate([eye, wt, eye]),
        "rows": np.stack([a["L3_cond_resp_b"], a["L3_cond_safety_bias"], a["L2_cond_up_b"]]).reshape(1, 3, D),
        "ln_rows": np.stack([a["L2_cond_ln_gamma"], a["L2_cond_ln_beta"]]),
        "const_f": const, "tokmask": tokmask, "params": np.concatenate(params, axis=1),
    }
    nc = bacc.Bacc("TRN2", target_bir_lowering=False, num_devices=1)
    arrays, args = {}, {}
    for name, v in ins.items():
        v = np.ascontiguousarray(v)
        arrays[f"in_{name}"] = v
        args[name] = nc.dram_tensor(f"in_{name}", v.shape, mybir.dt.from_np(v.dtype), kind="ExternalInput").ap()
    out = nc.dram_tensor("out_0", (B, S, D), mybir.dt.float32, kind="ExternalOutput").ap()
    cond_seq_program(nc, out=out, param_at=param_at, **args)
    r = run_bass_kernel_spmd(nc, [arrays], core_ids=[0])
    return r.results[0]["out_0"]
```
